# Optimizing a Trainium2 kernel written in Bass

```python
import numpy as np
import jax
import jax.numpy as jnp

def _softmax(x, axis=-1):
    return jax.nn.softmax(x, axis=axis)

def _gelu(x):
    return jax.nn.gelu(x, approximate=True)

def _silu(x):
    return jax.nn.silu(x)

def _sigmoid(x):
    return jax.nn.sigmoid(x)

def _layernorm(x, axis=-1, eps=1e-05):
    m = jnp.mean(x, axis=axis, keepdims=True)
    v = jnp.var(x, axis=axis, keepdims=True)
    return (x - m) / jnp.sqrt(v + eps)

def _scatter_add(tgt, idx, src, axis=0):
    return tgt.at[idx].add(src)

def _segment_sum(src, seg, n):
    return jax.ops.segment_sum(src, seg, n)
kernel_name = 'mk_gnn_preln_d2_gnn_r64_2a3422'

def setup_inputs(seed: int=0):
    np.random.seed(seed)
    _w = jnp.asarray

    def _rec_inputs():
        import jax
        import jax.numpy as jnp
        _gk = jax.random.key(seed)
        x = -0.0003713 + 1 * jax.random.normal(jax.random.fold_in(_gk, 1), (100000, 128), jnp.float32)
        src = jax.random.randint(jax.random.fold_in(_gk, 2), (50000,), 0, 100000, jnp.int32)
        dst = jax.random.randint(jax.random.fold_in(_gk, 3), (50000,), 0, 100000, jnp.int32)
        _o = jnp.argsort(dst, stable=True)
        src = src[_o]
        dst = dst[_o]
        edge_weight = jax.random.uniform(jax.random.fold_in(_gk, 12), (50000,), jnp.float32, 0.0, 0.999998)
        return (x, src, dst, edge_weight)
    x, src, dst, edge_weight = _rec_inputs()

    def _L0_gnn_setup():
        import jax, jax.numpy as jnp
        import numpy as np
        NEG_SLOPE = 0.2
        EPS = 1e-16
        N_NODES = 100000
        N_EDGES = 25000
        CHANNELS = 128
        M_LAYERS = 3

        def _gat_conv(x, src, dst, W, a_src, a_dst, b, n_nodes):
            h = x @ W
            s = h @ a_src
            d = h @ a_dst
            e = s[src] + d[dst]
            e = jnp.where(e > 0, e, NEG_SLOPE * e)
            e_max = jax.ops.segment_max(e, dst, num_segments=n_nodes)
            e_max = jnp.where(jnp.isfinite(e_max), e_max, 0.0)
            w = jnp.exp(e - e_max[dst])
            denom = jax.ops.segment_sum(w, dst, num_segments=n_nodes)
            alpha = w / (denom[dst] + EPS)
            out = jax.ops.segment_sum(alpha[:, None] * h[src], dst, num_segments=n_nodes)
            return out + b
        key = jax.random.key(seed)
        k1, k2, k3, k4, k5 = jax.random.split(key, 5)
        x = jax.random.normal(k1, (N_NODES, CHANNELS), dtype=jnp.float32)
        edge_index = jax.random.randint(k2, (2, N_EDGES), 0, N_NODES, dtype=jnp.int64)
        Ws = jax.random.normal(k3, (M_LAYERS, CHANNELS, CHANNELS), dtype=jnp.float32) / np.sqrt(CHANNELS)
        att_src = jax.random.normal(k4, (M_LAYERS, CHANNELS), dtype=jnp.float32) / np.sqrt(CHANNELS)
        att_dst = jax.random.normal(k5, (M_LAYERS, CHANNELS), dtype=jnp.float32) / np.sqrt(CHANNELS)
        bias = jnp.zeros((M_LAYERS, CHANNELS), dtype=jnp.float32)
        return {'x': x, 'edge_index': edge_index, 'Ws': Ws, 'att_src': att_src, 'att_dst': att_dst, 'bias': bias}
    _L0_gnn_all = _L0_gnn_setup()
    _L0_gnn_in = {k: v for k, v in _L0_gnn_all.items() if k in ('Ws', 'att_src', 'att_dst', 'bias')}
    del _L0_gnn_all

    def _L1_gnn_setup():
        import jax, jax.numpy as jnp
        import numpy as np
        N = 50000
        E = 12500
        D = 128

        def _glorot(key, shape):
            fan_in = shape[0]
            return jax.random.normal(key, shape, dtype=jnp.float32) * (1.0 / np.sqrt(fan_in))

        def _gnn_layer(edge_index, x, edge_attr, norm, We, be, Wn, bn):
            src, dst = (edge_index[0], edge_index[1])
            parts = [x[src], x[dst]]
            if edge_attr is not None:
                parts.append(edge_attr)
            e = jax.nn.relu(jnp.concatenate(parts, axis=-1) @ We + be)
            msg = e * norm[:, None] if norm is not None else e
            agg = jax.ops.segment_sum(msg, dst, num_segments=x.shape[0])
            x_new = jax.nn.relu(jnp.concatenate([x, agg], axis=-1) @ Wn + bn)
            return (x_new, e)
        key = jax.random.key(seed)
        ks = jax.random.split(key, 16)
        inp = {'edge_index': jax.random.randint(ks[0], (2, E), 0, N, dtype=jnp.int64), 'z': jax.random.normal(ks[1], (N, D), dtype=jnp.float32), 'norm': jax.random.uniform(ks[2], (E,), dtype=jnp.float32), 'We0': _glorot(ks[3], (2 * D, D)), 'be0': jnp.zeros((D,), jnp.float32), 'Wn0': _glorot(ks[4], (2 * D, D)), 'bn0': jnp.zeros((D,), jnp.float32), 'We1': _glorot(ks[5], (3 * D, D)), 'be1': jnp.zeros((D,), jnp.float32), 'Wn1': _glorot(ks[6], (2 * D, D)), 'bn1': jnp.zeros((D,), jnp.float32), 'We2': _glorot(ks[7], (3 * D, D)), 'be2': jnp.zeros((D,), jnp.float32), 'Wn2': _glorot(ks[8], (2 * D, D)), 'bn2': jnp.zeros((D,), jnp.float32)}
        return inp
    _L1_gnn_all = _L1_gnn_setup()
    _L1_gnn_in = {k: v for k, v in _L1_gnn_all.items() if k in ('We0', 'be0', 'Wn0', 'bn0', 'We1', 'be1', 'Wn1', 'bn1', 'We2', 'be2', 'Wn2', 'bn2')}
    del _L1_gnn_all
    return {'x': x, 'src': src, 'dst': dst, 'edge_weight': edge_weight, 'L0_gnn_Ws': _L0_gnn_in['Ws'], 'L0_gnn_att_src': _L0_gnn_in['att_src'], 'L0_gnn_att_dst': _L0_gnn_in['att_dst'], 'L0_gnn_bias': _L0_gnn_in['bias'], 'L1_gnn_We0': _L1_gnn_in['We0'], 'L1_gnn_be0': _L1_gnn_in['be0'], 'L1_gnn_Wn0': _L1_gnn_in['Wn0'], 'L1_gnn_bn0': _L1_gnn_in['bn0'], 'L1_gnn_We1': _L1_gnn_in['We1'], 'L1_gnn_be1': _L1_gnn_in['be1'], 'L1_gnn_Wn1': _L1_gnn_in['Wn1'], 'L1_gnn_bn1': _L1_gnn_in['bn1'], 'L1_gnn_We2': _L1_gnn_in['We2'], 'L1_gnn_be2': _L1_gnn_in['be2'], 'L1_gnn_Wn2': _L1_gnn_in['Wn2'], 'L1_gnn_bn2': _L1_gnn_in['bn2']}

def reference(x, src, dst, edge_weight, L0_gnn_Ws, L0_gnn_att_src, L0_gnn_att_dst, L0_gnn_bias, L1_gnn_We0, L1_gnn_be0, L1_gnn_Wn0, L1_gnn_bn0, L1_gnn_We1, L1_gnn_be1, L1_gnn_Wn1, L1_gnn_bn1, L1_gnn_We2, L1_gnn_be2, L1_gnn_Wn2, L1_gnn_bn2):
    import jax
    import jax.numpy as jnp

    def _L0_gnn_ref(x, edge_index, Ws, att_src, att_dst, bias):
        import jax, jax.numpy as jnp
        import numpy as np
        NEG_SLOPE = 0.2
        EPS = 1e-16
        N_NODES = 100000
        N_EDGES = 25000
        CHANNELS = 128
        M_LAYERS = 3

        def _gat_conv(x, src, dst, W, a_src, a_dst, b, n_nodes):
            h = x @ W
            s = h @ a_src
            d = h @ a_dst
            e = s[src] + d[dst]
            e = jnp.where(e > 0, e, NEG_SLOPE * e)
            e_max = jax.ops.segment_max(e, dst, num_segments=n_nodes)
            e_max = jnp.where(jnp.isfinite(e_max), e_max, 0.0)
            w = jnp.exp(e - e_max[dst])
            denom = jax.ops.segment_sum(w, dst, num_segments=n_nodes)
            alpha = w / (denom[dst] + EPS)
            out = jax.ops.segment_sum(alpha[:, None] * h[src], dst, num_segments=n_nodes)
            return out + b
        n = x.shape[0]
        loop = jnp.arange(n, dtype=edge_index.dtype)
        src = jnp.concatenate([edge_index[0], loop])
        dst = jnp.concatenate([edge_index[1], loop])
        for m in range(Ws.shape[0]):
            x = x + jax.nn.sigmoid(_gat_conv(x, src, dst, Ws[m], att_src[m], att_dst[m], bias[m], n))
        return x

    def _L1_gnn_ref(edge_index, z, norm, We0, be0, Wn0, bn0, We1, be1, Wn1, bn1, We2, be2, Wn2, bn2):
        import jax, jax.numpy as jnp
        import numpy as np
        N = 50000
        E = 12500
        D = 128

        def _glorot(key, shape):
            fan_in = shape[0]
            return jax.random.normal(key, shape, dtype=jnp.float32) * (1.0 / np.sqrt(fan_in))

        def _gnn_layer(edge_index, x, edge_attr, norm, We, be, Wn, bn):
            src, dst = (edge_index[0], edge_index[1])
            parts = [x[src], x[dst]]
            if edge_attr is not None:
                parts.append(edge_attr)
            e = jax.nn.relu(jnp.concatenate(parts, axis=-1) @ We + be)
            msg = e * norm[:, None] if norm is not None else e
            agg = jax.ops.segment_sum(msg, dst, num_segments=x.shape[0])
            x_new = jax.nn.relu(jnp.concatenate([x, agg], axis=-1) @ Wn + bn)
            return (x_new, e)
        x, edge_attr = _gnn_layer(edge_index, z, None, norm, We0, be0, Wn0, bn0)
        x, edge_attr = _gnn_layer(edge_index, x, edge_attr, norm, We1, be1, Wn1, bn1)
        x, edge_attr = _gnn_layer(edge_index, x, edge_attr, norm, We2, be2, Wn2, bn2)
        return x
    edge_index = jnp.stack([src, dst])
    h = jnp.maximum(_layernorm(x, axis=-1), 0.0)
    x = x + _L0_gnn_ref(h, edge_index, L0_gnn_Ws, L0_gnn_att_src, L0_gnn_att_dst, L0_gnn_bias)
    h = jnp.maximum(_layernorm(x, axis=-1), 0.0)
    x = x + _L1_gnn_ref(edge_index, h, edge_weight, L1_gnn_We0, L1_gnn_be0, L1_gnn_Wn0, L1_gnn_bn0, L1_gnn_We1, L1_gnn_be1, L1_gnn_Wn1, L1_gnn_bn1, L1_gnn_We2, L1_gnn_be2, L1_gnn_Wn2, L1_gnn_bn2)
    return x

_drawn_inputs = setup_inputs


def setup_inputs(seed=0):
    import zlib

    import numpy as np

    out = dict(_drawn_inputs(seed))
    spreads = {'L0_gnn_bias': (0.0, 0.549),
     'L1_gnn_be0': (0.0, 0.8),
     'L1_gnn_bn0': (0.0, 0.8),
     'L1_gnn_be1': (0.0, 0.8),
     'L1_gnn_bn1': (0.0, 2.0),
     'L1_gnn_be2': (0.0, 2.0),
     'L1_gnn_bn2': (0.0, 2.0)}
    factors = {'edge_weight': 4.354,
     'L0_gnn_att_src': 6.411,
     'L0_gnn_att_dst': 55.159,
     'L1_gnn_We0': 3.938,
     'L1_gnn_We1': 3.498,
     'L1_gnn_We2': 3.83}
    for name, (base, spread) in spreads.items():
        noise = np.random.default_rng([zlib.crc32(name.encode()), seed]).standard_normal(out[name].shape)
        drawn = base * np.exp(spread * noise) if base else spread * noise
        out[name] = jnp.asarray(drawn.astype(out[name].dtype))
    for name, factor in factors.items():
        out[name] = (out[name] * factor).astype(out[name].dtype)
    return out
```

```python
import numpy as np
import concourse.bass as bass
from concourse import mybir
from contextlib import ExitStack

N = 100000
E = 50000
C = 128
P = 128
U = 4
GE = -(-E // (P * U))
EP = GE * P * U
EF = E // (P * U)
ER = E - EF * P * U
NB = GE * U * 2
BJ = 7
BP = NB // BJ
ROWS = EP + NB + N
NODE0 = EP + NB
W0 = 132
GN = N // (P * U)
TAIL = N - GN * P * U
TP, TU = 80, 2
assert BP * BJ == NB and TP * TU == TAIL and BP <= P
LAYERS = 3
SKIP = 1 << 18
FAR = 1.0e30
EPS = 1e-5
SLOPE = 0.2
NF = 12
(DST, NORM, KEEP, CARRIED, SRCI, DSTI, OUTI, MAPI, MAPV) = range(9)
UE = 4
UD = 2


class Turn:

    def __init__(self, i, c, un, base=0):
        self.i, self.c, self.un, self.base = i, c, un, base
        self.slot = c % un

    def value(self, c, per_turn):
        return c if self.i is None else self.i * per_turn + c

    def count(self, more=1):
        return self.value(self.c + more, self.un)

    def uses(self, more=1, each=16, since=0, before=0):
        first = since + (self.slot - since) % self.un
        return self.value(((self.c - first) // self.un + before + more) * each, each)

    def part_uses(self, n, more=1, each=16):
        return self.value((self.c // n + more) * each, self.un // n * each)

    def at(self, size):
        return self.value((self.c - self.base) * size, self.un * size)


def uses_before(since, slot):
    return len([g for g in range(since, since + GE) if g % UE == slot])


def pipeline(eng, groups, work, un, base=0, last_peeled=0):
    low = min(lag for lag, _ in work)
    work = [(lag - low, fn) for lag, fn in work]
    depth = max(lag for lag, _ in work)
    first = depth + un
    turns = (groups - last_peeled - first) // un

    def step(s, i):
        for lag, fn in work:
            g = s - lag
            if i is not None or 0 <= g < groups:
                fn(Turn(i, g + base, un, base))

    for s in range(first):
        step(s, None)
    with eng.Fori(0, turns) as i:
        for k in range(un):
            step(first + k, i)
    for s in range(first + turns * un, groups + depth):
        step(s, None)


def after(eng, sem, g, back=1):
    if g.i is not None or g.c >= back:
        eng.wait_ge(sem, g.count(1 - back))


def after_part(eng, sem, g, n):
    if g.i is not None or g.c >= n:
        eng.wait_ge(sem, g.part_uses(n, 0))


def after_dma(eng, sem, g, each=16, since=0):
    if g.i is not None or g.c - since >= g.un:
        eng.wait_ge(sem, g.uses(0, each, since))


def build(nc, x, edges, edge_w, dst_rows, src_lookups, bnd_rows, bnd_cols, bnd_numbers, slot_numbers, node_numbers,
          tail_numbers, eye, gat_w_in, gat_wt_in, att_in, gat_b_in, node_b_in, edge_b_in, bias_rows_in,
          We0, Wn0, We1, Wn1, We2, Wn2, out):
    f32, i32, bf16 = mybir.dt.float32, mybir.dt.int32, mybir.dt.bfloat16
    ALU, ACT = mybir.AluOpType, mybir.ActivationFunctionType
    V, S, T, Q = nc.vector, nc.scalar, nc.tensor, nc.gpsimd
    ds = bass.ds
    NT = GE * U

    def dram(name, shape, dt=f32):
        return nc.dram_tensor(name, shape, dt, kind="Internal").ap()

    tables = [dram("table0", [N, W0])] + [dram(f"table{l}", [ROWS, C]) for l in range(1, 2 * LAYERS)]
    own0 = dram("own0", [EP + NB, C])
    raw_rows = dram("raw_rows", [EP, C])
    mid_rows = dram("mid_rows", [EP, C])
    mid_nodes = dram("mid_nodes", [N, C])
    records = dram("records", [GE, P, U * NF])
    lookups = dram("lookups", [GE, P, U], i32)
    bmasks = dram("bmasks", [GE, 2, U * P])
    bstats = dram("bstats", [2, NB])
    edge_feats = dram("edge_feats", [GE, C, U * P])

    with ExitStack() as ctx:
        def sb(name, shape, dt=f32, c=None):
            return (c or ctx).enter_context(nc.sbuf_tensor(name, shape, dt))

        settled = {}
        in_phase = []

        def sem(name):
            in_phase.append(nc.alloc_semaphore(name=name))
            return in_phase[-1]

        def end_phase():
            nc.clear_and_free_semaphores(in_phase)
            in_phase.clear()
            nc.all_engine_barrier()


        def settle(eng):
            if eng.engine not in settled:
                settled[eng.engine] = nc.alloc_semaphore(name=f"settled_{len(settled)}")
            eng.sem_inc(settled[eng.engine], 1)

        def sems(name, n=4):
            return [sem(f"{name}{k}") for k in range(n)]

        banks = [ctx.enter_context(nc.psum_tensor(f"bank{k}", [P, U, P], f32)) for k in range(8)]
        flat_banks = [b[:, :, :].rearrange("p u e -> p (u e)") for b in banks]

        ident = sb("ident", [P, P])
        ones3 = sb("ones3", [3, P], bf16)
        gat_w = sb("gat_w", [C, LAYERS, C])
        gat_b = sb("gat_b", [C, LAYERS])
        edge_b = sb("edge_b", [C, LAYERS])
        node_b = sb("node_b", [C, LAYERS])
        v_src = sb("v_src", [P, LAYERS, C])
        v_dst = sb("v_dst", [P, LAYERS, C])
        v_sum = sb("v_sum", [P, LAYERS, C])
        we = [sb(f"we{l}", [C, 2 + (l > 0), C]) for l in range(LAYERS)]
        wn = [sb(f"wn{l}", [C, 2, C]) for l in range(LAYERS)]
        brow3 = [sb(f"brow3_{l}", [3, U, C], bf16) for l in range(2 * LAYERS)]
        far = sb("far", [BP, BJ, NB])
        same = sb("same", [BP, BJ, NB])
        bexp = sb("bexp", [C, NB])
        braw = sb("braw", [BP, BJ, C])
        bout = sb("bout", [BP, BJ], i32)
        bclip = sb("bclip", [BP, BJ], i32)
        bmapi = sb("bmapi", [BP, BJ], i32)
        bmapv = sb("bmapv", [BP, BJ, 4])

        s_cl = sem("constants_loaded")
        s_el = sem("edges_loaded")
        s_dv = sem("setup_vector_step")
        s_pe = sem("products_ready")
        s_st = sem("setup_stored")
        with ExitStack() as c1:
            wT = sb("wT", [C, LAYERS, C], f32, c1)
            att = sb("att", [C, 2 * LAYERS], f32, c1)
            bias_rows = sb("bias_rows", [3, 2 * LAYERS, C], f32, c1)
            brest = sb("brest", [3, 2 * LAYERS, C], f32, c1)
            part = [sb(f"bpart{k}", [3, 2 * LAYERS, C], bf16, c1) for k in range(3)]
            edge_i = sb("edge_i", [P, 6, NT], i32, c1)
            edge_f = sb("edge_f", [P, 6, NT], f32, c1)
            wcol = sb("wcol", [P, NT], f32, c1)
            slots = sb("slots", [P, NT], f32, c1)
            tmp = sb("tmp", [P, 5, NT], f32, c1)
            rec = sb("rec", [P, NT, NF], f32, c1)
            row_i = sb("row_i", [GE, U, P], i32, c1)
            row_f = sb("row_f", [GE, U, P], f32, c1)
            row_m = sb("row_m", [GE, 3, U, P], f32, c1)
            brow_i = sb("brow_i", [BP, NB], i32, c1)
            brow_f = sb("brow_f", [BP, NB], f32, c1)
            bcol_i = sb("bcol_i", [BP, 3, BJ], i32, c1)
            bcol = sb("bcol", [BP, 3, BJ], f32, c1)
            btmp = sb("btmp", [BP, 3, BJ], f32, c1)
            f_dst, f_src, f_nxt, f_first, f_last, f_prev = (edge_f[:, k, :] for k in range(6))
            rec_i = rec[:, :, :].bitcast(i32)
            consts = [(ident[:, :], eye), (gat_w[:, :, :], gat_w_in), (wT[:, :, :], gat_wt_in),
                      (att[:, :], att_in), (gat_b[:, :], gat_b_in), (node_b[:, :], node_b_in),
                      (edge_b[:, :], edge_b_in), (bias_rows[:, :, :], bias_rows_in)]
            for l, (a, b) in enumerate(((We0, Wn0), (We1, Wn1), (We2, Wn2))):
                consts += [(we[l][:, :, :], a.rearrange("(k p) c -> p k c", p=C)),
                           (wn[l][:, :, :], b.rearrange("(k p) c -> p k c", p=C))]
            edge_loads = [(edge_i[:, :, :], edges), (wcol[:, :], edge_w), (slots[:, :], slot_numbers),
                          (row_i[:, :, :], dst_rows), (bcol_i[:, :, :], bnd_cols),
                          (brow_i[:, :], bnd_rows.broadcast_to([BP, NB])), (bmapv[:, :, 0], bnd_numbers)]
            mark = {}
            with nc.Block() as block:
                @block.vector
                def _(v):
                    n = [0]

                    def do(ins):
                        n[0] += 1
                        ins.then_inc(s_dv, 1)

                    def seen():
                        v.wait_ge(s_dv, n[0])

                    do(V.memset(ones3[:, :], 1.0))
                    do(V.memset(rec[:, :, :], 0.0))
                    do(V.memset(bmapv[:, :, :], 0.0))
                    mark["cleared"] = n[0]
                    v.wait_ge(s_el, 16 * len(edge_loads))
                    do(V.tensor_copy(edge_f[:, :, :], edge_i[:, :, :]))
                    do(V.tensor_copy(row_f[:, :, :], row_i[:, :, :]))
                    do(V.tensor_copy(bcol[:, :, :], bcol_i[:, :, :]))
                    do(V.tensor_copy(brow_f[:, :], brow_i[:, :]))
                    seen()
                    do(V.tensor_tensor(row_m[:, 0, :, :], row_f[:, :, :],
                                       row_f[:, :, 0:1].broadcast_to([GE, U, P]), ALU.is_equal))
                    do(V.tensor_tensor(row_m[:, 1, :, :], row_f[:, :, :],
                                       row_f[:, :, P - 1:P].broadcast_to([GE, U, P]), ALU.is_equal))
                    do(V.tensor_tensor(tmp[:, 0, :], f_dst, f_first, ALU.is_equal))
                    do(V.tensor_tensor(tmp[:, 1, :], f_dst, f_last, ALU.is_equal))
                    do(V.tensor_tensor(tmp[:, 2, :], f_dst, f_prev, ALU.is_equal))
                    do(V.tensor_tensor(tmp[:, 3, :], f_dst, f_nxt, ALU.not_equal))
                    do(V.tensor_scalar(tmp[:, 4, :], f_dst, -float(SKIP), None, ALU.add))
                    do(V.tensor_copy(rec[:, :, DST], f_dst))
                    do(V.tensor_copy(rec[:, :, NORM], wcol[:, :]))
                    do(V.tensor_copy(rec[:, :, MAPV], slots[:, :]))
                    do(V.tensor_copy(rec_i[:, :, SRCI], f_src))
                    seen()
                    do(V.tensor_scalar(f_first, f_dst, float(N - 1), None, ALU.min))
                    seen()
                    do(V.tensor_tensor(row_m[:, 2, :, :], row_m[:, 0, :, :], row_m[:, 1, :, :], ALU.mult))
                    do(V.tensor_tensor(tmp[:, 0, :], tmp[:, 0, :], tmp[:, 1, :], ALU.max))
                    do(V.tensor_tensor(tmp[:, 3, :], tmp[:, 3, :], tmp[:, 4, :], ALU.mult))
                    do(V.tensor_scalar(rec[:, :, CARRIED], tmp[:, 2, :], -FAR, None, ALU.mult))
                    do(V.tensor_copy(rec_i[:, :, DSTI], f_first))
                    seen()
                    do(V.tensor_tensor(row_m[:, 1, :, :], row_m[:, 1, :, :], row_m[:, 2, :, :], ALU.subtract))
                    do(V.tensor_scalar(tmp[:, 0, :], tmp[:, 0, :], -1.0, 1.0, ALU.mult, ALU.add))
                    seen()
                    mark["masks"] = n[0]
                    do(V.tensor_copy(rec[:, :, KEEP], tmp[:, 0, :]))
                    do(V.tensor_tensor(tmp[:, 3, :], tmp[:, 3, :], tmp[:, 0, :], ALU.mult))
                    seen()
                    do(V.tensor_scalar(tmp[:, 3, :], tmp[:, 3, :], float(SKIP), None, ALU.add))
                    seen()
                    do(V.tensor_copy(rec_i[:, :, OUTI], tmp[:, 3, :]))
                    do(V.tensor_scalar(tmp[:, 4, :], tmp[:, 3, :], float(W0 // 4), float(C // 4), ALU.mult, ALU.add))
                    seen()
                    do(V.tensor_copy(rec_i[:, :, MAPI], tmp[:, 4, :]))
                    mark["records"] = n[0]
                    do(V.tensor_tensor(btmp[:, 0, :], bcol[:, 0, :], bcol[:, 1, :], ALU.not_equal))
                    do(V.tensor_tensor(btmp[:, 1, :], bcol[:, 0, :], bcol[:, 2, :], ALU.not_equal))
                    do(V.tensor_scalar(btmp[:, 2, :], bcol[:, 0, :], -float(SKIP), None, ALU.add))
                    seen()
                    do(V.tensor_scalar(bcol[:, 2, :], bcol[:, 0, :], float(N - 1), None, ALU.min))
                    seen()
                    do(V.tensor_tensor(btmp[:, 2, :], btmp[:, 1, :], btmp[:, 2, :], ALU.mult))
                    do(V.tensor_copy(bclip[:, :], bcol[:, 2, :]))
                    seen()
                    do(V.tensor_scalar(btmp[:, 2, :], btmp[:, 2, :], float(SKIP), None, ALU.add))
                    seen()
                    do(V.tensor_copy(bout[:, :], btmp[:, 2, :]))
                    do(V.tensor_scalar(btmp[:, 1, :], btmp[:, 2, :], float(W0 // 4), float(C // 4), ALU.mult, ALU.add))
                    seen()
                    do(V.tensor_copy(bmapi[:, :], btmp[:, 1, :]))
                    for j in range(BJ):
                        do(V.tensor_scalar(far[:, j, :], brow_f[:, :], bcol[:, 0, j:j + 1], -FAR,
                                           ALU.not_equal, ALU.mult))
                        do(V.tensor_scalar(same[:, j, :], brow_f[:, :], bcol[:, 0, j:j + 1], btmp[:, 0, j:j + 1],
                                           ALU.is_equal, ALU.mult))
                    v.wait_ge(s_cl, 16 * len(consts))
                    do(V.tensor_copy(part[0][:, :, :], bias_rows[:, :, :]))
                    seen()
                    do(V.tensor_tensor(brest[:, :, :], bias_rows[:, :, :], part[0][:, :, :], ALU.subtract))
                    seen()
                    do(V.tensor_copy(part[1][:, :, :], brest[:, :, :]))
                    seen()
                    do(V.tensor_tensor(brest[:, :, :], brest[:, :, :], part[1][:, :, :], ALU.subtract))
                    seen()
                    do(V.tensor_copy(part[2][:, :, :], brest[:, :, :]))
                    seen()
                    do(V.tensor_scalar(brest[:, :, :], part[0][:, :, :], ident[0:3, 0:1], None, ALU.mult))
                    for k in (1, 2):
                        seen()
                        do(V.scalar_tensor_tensor(out=brest[:, :, :], in0=part[k][:, :, :], scalar=ident[0:3, k:k + 1],
                                                  in1=brest[:, :, :], op0=ALU.mult, op1=ALU.add))
                    seen()
                    for l in range(2 * LAYERS):
                        do(V.tensor_copy(brow3[l][:, :, :], brest[:, l:l + 1, :].broadcast_to([3, U, C])))
                    v.wait_ge(s_pe, 1)
                    do(V.tensor_copy(v_src[:, :, :], banks[0][:, 0:LAYERS, :]))
                    do(V.tensor_copy(v_dst[:, :, :], banks[1][:, 0:LAYERS, :]))
                    seen()
                    do(V.tensor_tensor(v_sum[:, :, :], v_src[:, :, :], v_dst[:, :, :], ALU.add))
                    seen()

                @block.tensor
                def _(pe):
                    pe.wait_ge(s_cl, 16 * len(consts))
                    for h in range(2):
                        for l in range(LAYERS):
                            k = h * LAYERS + l
                            last = T.matmul(banks[h][:, l, :], lhsT=att[:, k:k + 1].broadcast_to([C, P]),
                                            rhs=wT[:, l, :], start=True, stop=True)
                    last.then_inc(s_pe, 1)

                @block.sync
                def _(sp):
                    sp.wait_ge(s_dv, mark["cleared"])
                    with nc.allow_non_contiguous_dma("boundary numbers among padding"):
                        for to, of in edge_loads:
                            sp.dma_start(to, of).then_inc(s_el, 16)
                    for to, of in consts:
                        sp.dma_start(to, of).then_inc(s_cl, 16)
                    sp.wait_ge(s_dv, mark["masks"])
                    sp.dma_start(bmasks.rearrange("g r e -> g (r e)"),
                                 row_m[:, 0:2, :, :].rearrange("g r u e -> g (r u e)")).then_inc(s_st, 16)
                    sp.wait_ge(s_dv, mark["records"])
                    sp.dma_start(records.rearrange("g p w -> p g w"),
                                 rec[:, :, :].rearrange("p (g u) f -> p g (u f)", u=U)).then_inc(s_st, 16)
                    sp.wait_ge(s_st, 32)

        end_phase()

        def norm_sems(name):
            return {k: sem(f"{name}_{k}") for k in ("stats", "moments", "var", "root", "rstd", "shift", "done")}

        def norm_tiles(c, tag, n, u):
            return [dict(st=sb(f"{tag}_st{k}", [P, u, 6], f32, c), mv=sb(f"{tag}_mv{k}", [P, u, 2], f32, c),
                         sc=sb(f"{tag}_sc{k}", [P, 4, u], f32, c)) for k in range(n)]

        def norm_vector_a(v, z, t, rows, n, p, u):
            for k in range(u):
                last = V.bn_stats(t["st"][0:p, k, :], rows[0:p, k, :])
            last.then_inc(z["stats"], 1)
            v.wait_ge(z["stats"], n)
            settle(v)
            for k in range(u):
                last = V.bn_aggr(t["mv"][0:p, k, :], t["st"][0:p, k, :])
            last.then_inc(z["moments"], 1)
            v.wait_ge(z["moments"], n)
            V.tensor_scalar(t["sc"][0:p, 0, 0:u], t["mv"][0:p, 0:u, 1], EPS, None, ALU.add).then_inc(z["var"], 1)

        def norm_scalar_a(a, z, t, n, p, u):
            a.wait_ge(z["var"], n)
            S.activation(t["sc"][0:p, 1, 0:u], t["sc"][0:p, 0, 0:u], ACT.Sqrt).then_inc(z["root"], 1)

        def norm_vector_b(v, z, t, n, p, u):
            v.wait_ge(z["root"], n)
            V.reciprocal(t["sc"][0:p, 2, 0:u], t["sc"][0:p, 1, 0:u]).then_inc(z["rstd"], 1)
            v.wait_ge(z["rstd"], n)
            V.scalar_tensor_tensor(out=t["sc"][0:p, 3, 0:u], in0=t["mv"][0:p, 0:u, 0], scalar=-1.0,
                                   in1=t["sc"][0:p, 2, 0:u], op0=ALU.mult, op1=ALU.mult).then_inc(z["shift"], 1)

        def norm_scalar_b(a, z, t, rows, to, n, p, u):
            a.wait_ge(z["shift"], n)
            for k in range(u):
                last = S.activation(to[0:p, k, 0:C], rows[0:p, k, :], ACT.Relu,
                                    bias=t["sc"][0:p, 3, k:k + 1], scale=t["sc"][0:p, 2, k:k + 1])
            last.then_inc(z["done"], 1)

        def shape_of(g):
            return (TP, TU) if g.i is None and g.c - g.base == GN else (P, U)

        def node_rows(t, g, first=0):
            p, u = shape_of(g)
            return t[ds(g.at(P * U) + first, p * u), :].rearrange("(p u) c -> p u c", p=p)

        def slot_rows(t, g):
            return t[ds(g.at(P * U), P * U), :].rearrange("(p u) c -> p u c", p=P)

        def norm_pass(name, groups, load_from, store_to, width, un, peeled, numbers=None):
            z = norm_sems(name)
            z_ld, z_st = sems(f"{name}_loaded", un), sems(f"{name}_stored", un)
            z_nx, z_nc = sem(f"{name}_next_numbers"), sem(f"{name}_numbered")
            with ExitStack() as c2:
                t = norm_tiles(c2, name, un, U)
                rows = [sb(f"{name}_rows{k}", [P, U, C], f32, c2) for k in range(un)]
                h = [sb(f"{name}_h{k}", [P, U, width], f32, c2) for k in range(un)]
                num = sb(f"{name}_num", [P, U], f32, c2)
                tnum = sb(f"{name}_tnum", [P, TU], f32, c2)
                with nc.Block() as block:
                    @block.sync
                    def _(sp):
                        if numbers:
                            sp.dma_start(num[:, :], node_numbers).then_inc(z_nc, 16)
                            sp.dma_start(tnum[0:TP, :], tail_numbers).then_inc(z_nc, 16)

                        def load(g):
                            p, u = shape_of(g) if numbers else (P, U)
                            sp.wait_ge(z["done"], g.count())
                            settle(sp)
                            sp.dma_start(rows[g.slot][0:p, 0:u, :], load_from(g)).then_inc(z_ld[g.slot], 16)
                        pipeline(sp, groups, [(0, load)], un, last_peeled=peeled)

                    @block.gpsimd
                    def _(q):
                        q.sem_inc(z["done"], un)

                        def store(g):
                            p, u = shape_of(g) if numbers else (P, U)
                            q.wait_ge(z["done"], g.count(1 + un))
                            if numbers:
                                q.wait_ge(z_nx, g.count(2))
                            settle(q)
                            q.dma_start(store_to(g), h[g.slot][0:p, 0:u, :]).then_inc(z_st[g.slot], 16)
                        pipeline(q, groups, [(0, store)], un, last_peeled=peeled)
                        for k in range(un):
                            q.wait_ge(z_st[k], 16 * ((groups - k + un - 1) // un))

                    @block.vector
                    def _(v):
                        if numbers:
                            for k in range(un):
                                V.memset(h[k][:, :, C:width], 0.0)
                            v.wait_ge(z_nc, 32)
                            V.tensor_scalar(num[:, :], num[:, :], 0.0, None, ALU.add).then_inc(z_nx, 1)

                        def first(g):
                            p, u = shape_of(g) if numbers else (P, U)
                            v.wait_ge(z_ld[g.slot], g.uses())
                            norm_vector_a(v, z, t[g.slot], rows[g.slot], g.count(), p, u)

                        def second(g):
                            p, u = shape_of(g) if numbers else (P, U)
                            norm_vector_b(v, z, t[g.slot], g.count(), p, u)
                            if numbers:
                                after_dma(v, z_st[g.slot], g)
                                v.wait_ge(z_nx, g.count())
                                if p == P:
                                    V.tensor_copy(h[g.slot][:, :, C], num[:, :]).then_inc(z_nc, 1)
                                    v.wait_ge(z_nc, g.count(33))
                                    V.tensor_scalar(num[:, :], num[:, :], float(P * U), None, ALU.add)\
                                     .then_inc(z_nx, 1)
                                else:
                                    V.tensor_copy(h[g.slot][0:p, 0:u, C], tnum[0:p, 0:u]).then_inc(z_nx, 1)
                        pipeline(v, groups, [(1, second), (0, first)], un, last_peeled=peeled)

                    @block.scalar
                    def _(a):
                        def first(g):
                            norm_scalar_a(a, z, t[g.slot], g.count(), *(shape_of(g) if numbers else (P, U)))

                        def second(g):
                            after_dma(a, z_st[g.slot], g)
                            norm_scalar_b(a, z, t[g.slot], rows[g.slot], h[g.slot], g.count(),
                                          *(shape_of(g) if numbers else (P, U)))
                        pipeline(a, groups, [(1, second), (0, first)], un, last_peeled=peeled)

        norm_pass("nodes_norm", GN + 1, lambda g: node_rows(x, g), lambda g: node_rows(tables[0], g),
                  W0, 4, 1, numbers=True)

        end_phase()

        z = norm_sems("edges_norm")
        x_es, x_gx, x_st, x_mp = sems("x_records"), sems("x_gathered"), sems("x_stored"), sems("x_mapped")
        with ExitStack() as c2:
            t = norm_tiles(c2, "edges_norm", UE, U)
            es = [sb(f"x_es{k}", [P, U, NF], f32, c2) for k in range(UE)]
            rows = [sb(f"x_rows{k}", [P, U, C], f32, c2) for k in range(UE)]
            h = [sb(f"x_h{k}", [P, U, C], f32, c2) for k in range(UE)]
            map_view = tables[0].rearrange("n (a w) -> (n a) w", w=4)
            with nc.Block() as block:
                @block.sync
                def _(sp):
                    def load(g):
                        after_dma(sp, x_mp[g.slot], g, 16 * U)
                        settle(sp)
                        sp.dma_start(es[g.slot][:, :, :], records[ds(g.at(1), 1), :, :].rearrange(
                            "a p w -> (a p) w")).then_inc(x_es[g.slot], 16)

                    def store(g):
                        sp.wait_ge(x_gx[g.slot], g.uses(1, 16 * U))
                        settle(sp)
                        sp.dma_start(slot_rows(raw_rows, g), rows[g.slot][:, :, :]).then_inc(x_st[g.slot], 16)
                        sp.wait_ge(z["done"], g.count())
                        settle(sp)
                        sp.dma_start(slot_rows(own0, g), h[g.slot][:, :, :]).then_inc(x_st[g.slot], 16)
                    pipeline(sp, GE, [(2, store), (0, load)], UE)
                    for k in range(UE):
                        sp.wait_ge(x_st[k], 32 * ((GE - k + UE - 1) // UE))

                @block.gpsimd
                def _(q):
                    def first(g):
                        b = g.slot
                        after_dma(q, x_st[b], g, 32)
                        q.wait_ge(x_es[b], g.uses())
                        settle(q)
                        for u in range(U):
                            q.indirect_dma_start(
                                out=rows[b][:, u, :], out_offset=None, in_=x,
                                in_offset=bass.IndirectOffsetOnAxis(
                                    ap=es[b][:, u, DSTI:DSTI + 1].bitcast(i32), axis=0),
                                bounds_check=N - 1, oob_is_err=False).then_inc(x_gx[b], 16)
                        for u in range(U):
                            q.indirect_dma_start(
                                out=map_view, out_offset=bass.IndirectOffsetOnAxis(
                                    ap=es[b][:, u, MAPI:MAPI + 1].bitcast(i32), axis=0),
                                in_=es[b][:, u, MAPV:NF], in_offset=None,
                                bounds_check=N * (W0 // 4) - 1, oob_is_err=False).then_inc(x_mp[b], 16)
                    pipeline(q, GE, [(0, first)], UE)
                    for k in range(UE):
                        q.wait_ge(x_mp[k], 16 * U * ((GE - k + UE - 1) // UE))

                @block.vector
                def _(v):
                    def first(g):
                        v.wait_ge(x_gx[g.slot], g.uses(1, 16 * U))
                        norm_vector_a(v, z, t[g.slot], rows[g.slot], g.count(), P, U)

                    def second(g):
                        norm_vector_b(v, z, t[g.slot], g.count(), P, U)
                    pipeline(v, GE, [(1, second), (0, first)], UE)

                @block.scalar
                def _(a):
                    def first(g):
                        norm_scalar_a(a, z, t[g.slot], g.count(), P, U)

                    def second(g):
                        after_dma(a, x_st[g.slot], g, 32)
                        norm_scalar_b(a, z, t[g.slot], rows[g.slot], h[g.slot], g.count(), P, U)
                    pipeline(a, GE, [(1, second), (0, first)], UE)

        end_phase()

        zb = norm_sems("boundary_norm")
        b_gx, b_st = sem("boundary_gathered"), sem("boundary_stored")
        with ExitStack() as c2:
            tbn = norm_tiles(c2, "boundary_norm", 1, BJ)[0]
            hb = sb("boundary_h", [BP, BJ, C], f32, c2)

            def boundary_rows(table, first):
                return table[first:first + NB, :].rearrange("(j p) c -> p j c", p=BP)

            with nc.Block() as block:
                @block.gpsimd
                def _(q):
                    for j in range(BJ):
                        q.indirect_dma_start(
                            out=braw[:, j, :], out_offset=None, in_=x,
                            in_offset=bass.IndirectOffsetOnAxis(ap=bclip[:, j:j + 1], axis=0),
                            bounds_check=N - 1, oob_is_err=False).then_inc(b_gx, 16)
                    for j in range(BJ):
                        q.indirect_dma_start(
                            out=map_view, out_offset=bass.IndirectOffsetOnAxis(ap=bmapi[:, j:j + 1], axis=0),
                            in_=bmapv[:, j, :], in_offset=None,
                            bounds_check=N * (W0 // 4) - 1, oob_is_err=False).then_inc(b_st, 16)
                    q.wait_ge(zb["done"], 1)
                    settle(q)
                    q.dma_start(boundary_rows(own0, EP), hb[:, :, :]).then_inc(b_st, 16)
                    q.wait_ge(b_st, 16 * (BJ + 1))

                @block.vector
                def _(v):
                    v.wait_ge(b_gx, 16 * BJ)
                    norm_vector_a(v, zb, tbn, braw, 1, BP, BJ)
                    norm_vector_b(v, zb, tbn, 1, BP, BJ)

                @block.scalar
                def _(a):
                    norm_scalar_a(a, zb, tbn, 1, BP, BJ)
                    norm_scalar_b(a, zb, tbn, braw, hb, 1, BP, BJ)

        end_phase()

        d_ld, d_xl, d_st = sems("d_loaded", 4), sems("d_x_loaded", 4), [sems(f"d_stored{m}_", 2) for m in range(3)]
        d_t0, d_c0 = sem("d_transposed"), sem("d_copied")
        d_mm, d_sg, d_ad, d_tr, d_rw = (sems(f"d_{k}", 3) for k in ("product", "gate", "added", "back", "rows"))
        with ExitStack() as c2:
            rows = [sb(f"d_rows{k}", [P, U, C], f32, c2) for k in range(4)]
            xr = [sb(f"d_xr{k}", [P, U, C], f32, c2) for k in range(4)]
            xT = [[sb(f"d_xT{m}_{k}", [C, U, P], f32, c2) for k in range(2)] for m in range(4)]
            sg = [[sb(f"d_sg{m}_{k}", [C, U, P], f32, c2) for k in range(2)] for m in range(3)]
            ro = [[sb(f"d_ro{m}_{k}", [P, U, C], f32, c2) for k in range(2)] for m in range(3)]
            def node_out(m, g):
                return node_rows(mid_nodes, g) if m == 2 else node_rows(tables[m + 1], g, NODE0)

            with nc.Block() as block:
                @block.sync
                def _(sp):
                    def load(g):
                        p, u = shape_of(g)
                        sp.wait_ge(d_t0, g.count())
                        settle(sp)
                        sp.dma_start(rows[g.slot][0:p, 0:u, :], node_rows(tables[0], g)[:, :, 0:C])\
                          .then_inc(d_ld[g.slot], 16)
                        sp.wait_ge(d_rw[2], g.count())
                        settle(sp)
                        sp.dma_start(xr[g.slot][0:p, 0:u, :], node_rows(x, g)).then_inc(d_xl[g.slot], 16)
                    sp.sem_inc(d_t0, 4)
                    sp.sem_inc(d_rw[2], 4)

                    def store(m):
                        def fn(g):
                            p, u = shape_of(g)
                            k = g.slot % 2
                            sp.wait_ge(d_rw[m], g.count(5 if m == 2 else 2))
                            settle(sp)
                            sp.dma_start(node_out(m, g), ro[m][k][0:p, 0:u, :]).then_inc(d_st[m][k], 16)
                        return fn
                    pipeline(sp, GN + 1, [(0, load)] + [(m + 2, store(m)) for m in (2, 1, 0)], 4, last_peeled=1)
                    for m in range(3):
                        for k in range(2):
                            sp.wait_ge(d_st[m][k], 16 * ((GN + 2 - k) // 2))

                @block.tensor
                def _(pe):
                    def enter(g):
                        p, u = shape_of(g)
                        pe.wait_ge(d_ld[g.slot], g.uses())
                        pe.wait_ge(d_c0, g.count())
                        for k in range(u):
                            last = T.transpose(banks[0][:, k, 0:p], rows[g.slot][0:p, k, :], ident[0:p, 0:p])
                        last.then_inc(d_t0, 1)

                    def product(m):
                        def fn(g):
                            p, u = shape_of(g)
                            pe.wait_ge(d_c0 if m == 0 else d_ad[m - 1], g.count(2 if m == 0 else 1))
                            pe.wait_ge(d_sg[m], g.count())
                            T.matmul(banks[1 + m][:, 0:u, 0:p], lhsT=gat_w[:, m, :],
                                     rhs=xT[m][g.slot % 2][:, 0:u, 0:p], start=True, stop=True)\
                             .then_inc(d_mm[m], 1)
                        return fn

                    def back(m):
                        def fn(g):
                            p, u = shape_of(g)
                            pe.wait_ge(d_ad[m], g.count())
                            pe.wait_ge(d_rw[m], g.count(1 if m < 2 else 4))
                            for k in range(u):
                                last = T.transpose(banks[4 + m][0:p, k, :], xT[m + 1][g.slot % 2][:, k, 0:p],
                                                   ident[:, :])
                            last.then_inc(d_tr[m], 1)
                        return fn
                    pipeline(pe, GN + 1, [(4, back(2)), (3, product(2)), (3, back(1)), (2, product(1)), (2, back(0)),
                              (1, product(0)), (0, enter)], 4, last_peeled=1)

                @block.scalar
                def _(a):
                    a.sem_inc(d_c0, 1)
                    for m in range(3):
                        a.sem_inc(d_sg[m], 1)

                    def enter(g):
                        p, u = shape_of(g)
                        a.wait_ge(d_t0, g.count(5))
                        S.activation(xT[0][g.slot % 2][:, 0:u, 0:p], banks[0][:, 0:u, 0:p], ACT.Copy)\
                         .then_inc(d_c0, 1)

                    def gate(m):
                        def fn(g):
                            p, u = shape_of(g)
                            a.wait_ge(d_mm[m], g.count())
                            S.activation(sg[m][g.slot % 2][:, 0:u, 0:p], banks[1 + m][:, 0:u, 0:p], ACT.Sigmoid,
                                         bias=gat_b[:, m:m + 1]).then_inc(d_sg[m], 1)
                        return fn
                    def rows0(g):
                        p, u = shape_of(g)
                        k = g.slot % 2
                        after_part(a, d_st[0][k], g, 2)
                        a.wait_ge(d_tr[0], g.count())
                        S.activation(ro[0][k][0:p, 0:u, :], banks[4][0:p, 0:u, :], ACT.Copy).then_inc(d_rw[0], 1)
                    a.sem_inc(d_rw[0], 1)
                    pipeline(a, GN + 1, [(3, gate(2)), (2, gate(1)), (2, rows0), (1, gate(0)), (0, enter)], 4,
                             last_peeled=1)

                @block.vector
                def _(v):
                    v.sem_inc(d_rw[1], 1)

                    def add(m):
                        def fn(g):
                            p, u = shape_of(g)
                            k = g.slot % 2
                            v.wait_ge(d_sg[m], g.count(2))
                            V.tensor_tensor(xT[m + 1][k][:, 0:u, 0:p], xT[m][k][:, 0:u, 0:p],
                                            sg[m][k][:, 0:u, 0:p], ALU.add).then_inc(d_ad[m], 1)
                        return fn

                    def rows_of(m):
                        def fn(g):
                            p, u = shape_of(g)
                            k = g.slot % 2
                            after_part(v, d_st[m][k], g, 2)
                            v.wait_ge(d_tr[m], g.count())
                            if m < 2:
                                V.tensor_copy(ro[m][k][0:p, 0:u, :], banks[4 + m][0:p, 0:u, :])\
                                 .then_inc(d_rw[m], 1)
                            else:
                                v.wait_ge(d_xl[g.slot], g.uses())
                                V.tensor_tensor(ro[m][k][0:p, 0:u, :], banks[4 + m][0:p, 0:u, :],
                                                xr[g.slot][0:p, 0:u, :], ALU.add).then_inc(d_rw[m], 1)
                        return fn
                    pipeline(v, GN + 1, [(4, rows_of(2)), (3, add(2)), (3, rows_of(1)), (2, add(1)),
                                         (1, add(0))], 4, last_peeled=1)

        end_phase()

        zc = norm_sems("c_norm")
        c_ld, c_st = sems("c_loaded", 8), [sems(f"c_stored{m}_", 2) for m in range(4)]
        c_t0, c_c0 = sem("c_transposed"), sem("c_copied")
        c_mm, c_re, c_tr, c_rw = (sems(f"c_{k}", 3) for k in ("product", "relu", "back", "rows"))
        with ExitStack() as c2:
            t = norm_tiles(c2, "c_norm", 8, U)
            rows = [sb(f"c_rows{k}", [P, U, C], f32, c2) for k in range(8)]
            zr = [sb(f"c_zr{k}", [P, U, C], f32, c2) for k in range(2)]
            zT = [[sb(f"c_zT{m}_{k}", [C, U, P], f32, c2) for k in range(2)] for m in range(4)]
            ro = [[sb(f"c_ro{m}_{k}", [P, U, C], f32, c2) for k in range(2)] for m in range(3)]

            with nc.Block() as block:
                @block.sync
                def _(sp):
                    sp.sem_inc(c_rw[2], 8)

                    def load(g):
                        p, u = shape_of(g)
                        sp.wait_ge(c_rw[2], g.count())
                        settle(sp)
                        sp.dma_start(rows[g.slot][0:p, 0:u, :], node_rows(mid_nodes, g)).then_inc(c_ld[g.slot], 16)

                    def store_norm(g):
                        p, u = shape_of(g)
                        sp.wait_ge(zc["done"], g.count())
                        settle(sp)
                        sp.dma_start(node_rows(tables[3], g, NODE0), zr[g.slot % 2][0:p, 0:u, :])\
                         .then_inc(c_st[3][g.slot % 2], 16)

                    def store(m):
                        def fn(g):
                            p, u = shape_of(g)
                            k = g.slot % 2
                            sp.wait_ge(c_rw[m], g.count(1 + 8 * (m == 2) + (m < 2)))
                            to = node_rows(out, g) if m == 2 else node_rows(tables[4 + m], g, NODE0)
                            settle(sp)
                            sp.dma_start(to, ro[m][k][0:p, 0:u, :]).then_inc(c_st[m][k], 16)
                        return fn
                    pipeline(sp, GN + 1, [(-2, load), (5, store(2)), (4, store(1)), (3, store(0)), (1, store_norm)], 8,
                             last_peeled=1)
                    for m in range(4):
                        for k in range(2):
                            sp.wait_ge(c_st[m][k], 16 * ((GN + 2 - k) // 2))

                @block.vector
                def _(v):
                    def first(g):
                        v.wait_ge(c_ld[g.slot], g.uses())
                        norm_vector_a(v, zc, t[g.slot], rows[g.slot], g.count(), *shape_of(g))

                    def second(g):
                        norm_vector_b(v, zc, t[g.slot], g.count(), *shape_of(g))

                    def rows_of(m):
                        def fn(g):
                            p, u = shape_of(g)
                            k = g.slot % 2
                            after_part(v, c_st[m][k], g, 2)
                            v.wait_ge(c_tr[m], g.count())
                            if m < 2:
                                V.tensor_copy(ro[m][k][0:p, 0:u, :], banks[4 + m][0:p, 0:u, :])\
                                 .then_inc(c_rw[m], 1)
                            else:
                                V.tensor_tensor(ro[m][k][0:p, 0:u, :], banks[4 + m][0:p, 0:u, :],
                                                rows[g.slot][0:p, 0:u, :], ALU.add).then_inc(c_rw[m], 1)
                        return fn

                    def enter(g):
                        p, u = shape_of(g)
                        v.wait_ge(c_t0, g.count())
                        V.tensor_copy(zT[0][g.slot % 2][:, 0:u, 0:p], banks[0][:, 0:u, 0:p]).then_inc(c_c0, 1)
                    v.sem_inc(c_c0, 1)
                    v.sem_inc(c_rw[0], 1)
                    v.sem_inc(c_rw[1], 1)
                    pipeline(v, GN + 1, [(5, rows_of(2)), (4, rows_of(1)), (3, rows_of(0)), (2, enter), (1, second),
                                         (0, first)], 8, last_peeled=1)

                @block.scalar
                def _(a):
                    for m in range(3):
                        a.sem_inc(c_re[m], 1)

                    def first(g):
                        norm_scalar_a(a, zc, t[g.slot], g.count(), *shape_of(g))

                    def second(g):
                        k = g.slot % 2
                        after_part(a, c_st[3][k], g, 2)
                        after(a, c_t0, g, 2)
                        norm_scalar_b(a, zc, t[g.slot], rows[g.slot], zr[k], g.count(), *shape_of(g))

                    def relu(m):
                        def fn(g):
                            p, u = shape_of(g)
                            a.wait_ge(c_mm[m], g.count())
                            S.activation(zT[m + 1][g.slot % 2][:, 0:u, 0:p], banks[1 + m][:, 0:u, 0:p], ACT.Relu,
                                         bias=node_b[:, m:m + 1]).then_inc(c_re[m], 1)
                        return fn
                    pipeline(a, GN + 1, [(4, relu(2)), (3, relu(1)), (2, relu(0)), (1, second), (0, first)], 8,
                             last_peeled=1)

                @block.tensor
                def _(pe):
                    def enter(g):
                        p, u = shape_of(g)
                        pe.wait_ge(zc["done"], g.count())
                        pe.wait_ge(c_c0, g.count())
                        for k in range(u):
                            last = T.transpose(banks[0][:, k, 0:p], zr[g.slot % 2][0:p, k, :], ident[0:p, 0:p])
                        last.then_inc(c_t0, 1)

                    def product(m):
                        def fn(g):
                            p, u = shape_of(g)
                            pe.wait_ge(c_c0 if m == 0 else c_re[m - 1], g.count(2))
                            pe.wait_ge(c_re[m], g.count())
                            T.matmul(banks[1 + m][:, 0:u, 0:p], lhsT=wn[m][:, 0, :],
                                     rhs=zT[m][g.slot % 2][:, 0:u, 0:p], start=True, stop=True)\
                             .then_inc(c_mm[m], 1)
                        return fn

                    def back(m):
                        def fn(g):
                            p, u = shape_of(g)
                            pe.wait_ge(c_re[m], g.count(2))
                            pe.wait_ge(c_rw[m], g.count(1 if m < 2 else 8))
                            for k in range(u):
                                last = T.transpose(banks[4 + m][0:p, k, :], zT[m + 1][g.slot % 2][:, k, 0:p],
                                                   ident[:, :])
                            last.then_inc(c_tr[m], 1)
                        return fn
                    pipeline(pe, GN + 1, [(5, back(2)), (4, product(2)), (4, back(1)), (3, product(1)), (3, back(0)),
                                          (2, product(0)), (1, enter)], 8, last_peeled=1)

        end_phase()

        def own_of(l):
            return own0 if l == 0 else tables[l]

        e_es, e_gi, e_xd, e_gx, e_ex = (sems(f"e_{k}") for k in ("records", "lookups", "own", "gathered", "extra"))
        e_st, e_bs, e_lk = sems("e_stored"), sems("e_bstats_stored"), sems("e_lookups_stored")

        def load_group(sp, g, l, t, extra=None):
            b = g.slot
            sp.dma_start(t["es"][b][:, :, :], records[ds(g.at(1), 1), :, :].rearrange("a p w -> (a p) w"))\
              .then_inc(e_es[b], 16)
            sp.dma_start(t["gi"][b][:, :], (src_lookups if l == 0 else lookups)[ds(g.at(1), 1), :, :].rearrange(
                "a p u -> (a p) u")).then_inc(e_gi[b], 16)
            own = own_of(l)
            sp.dma_start(t["xd"][b][:, :, :], slot_rows(own, g)).then_inc(e_xd[b], 16)
            sp.dma_start(t["b2"][b][:, :, :], own[ds(g.at(2 * U) + EP, 2 * U), :].rearrange(
                "(r u) c -> r u c", r=2)).then_inc(e_xd[b], 16)
            sp.dma_start(t["fm"][b][:, :, :], bmasks[ds(g.at(1), 1), :, :].rearrange(
                "a r (u e) -> (a r) u e", u=U)).then_inc(e_xd[b], 16)

        def gather_group(q, g, l, t):
            b = g.slot
            q.wait_ge(e_gi[b], g.uses())
            settle(q)
            width = W0 if l == 0 else C
            for u in range(U):
                q.indirect_dma_start(out=t["xs"][b][:, u, 0:width], out_offset=None, in_=tables[l],
                                     in_offset=bass.IndirectOffsetOnAxis(ap=t["gi"][b][:, u:u + 1], axis=0),
                                     bounds_check=(N if l == 0 else ROWS) - 1, oob_is_err=False)\
                 .then_inc(e_gx[b], 16)

        def tiles_of(c, tag, names):
            shapes = dict(es=([P, U, NF], f32), gi=([P, U], i32), xs=([P, U, W0], f32), b2=([2, U, C], f32),
                          fm=([2, U, P], f32), zz=([P, 2, U], f32), dd=([P, U], f32), ev=([P, 2, U], f32),
                          ml=([P, 2, U], f32), arg=([P, 2, U], f32), w=([P, 2, U], f32), rl=([P, U], f32),
                          al=([P, 2, U], f32), li=([P, U], i32))
            return {n: [sb(f"{tag}_{n}{k}", *shapes.get(n, ([P, U, P], f32)), c) for k in range(UE)] for n in names}

        def bc(ap):
            return ap.unsqueeze(2).broadcast_to([P, U, P])

        def tile_matrix_rows(pe, g, t):
            for u in range(U):
                last = T.transpose(banks[0][:, u, :], t["es"][g.slot][:, u, DST:DST + 1].broadcast_to([P, P]),
                                   ident[:, :])
            return last

        def boundary_values(pe, g, t):
            for u in range(U):
                last = T.matmul(banks[1][:, u, :], lhsT=t["fm"][g.slot][0:2, u, :], rhs=t["b2"][g.slot][0:2, u, :],
                                start=True, stop=True)
            return last

        def put_boundary_values(v, g, t):
            for u in range(U):
                last = V.scalar_tensor_tensor(out=t["xd"][g.slot][:, u, :], in0=t["xd"][g.slot][:, u, :],
                                              scalar=t["es"][g.slot][:, u, KEEP:KEEP + 1], in1=banks[1][:, u, :],
                                              op0=ALU.mult, op1=ALU.add)
            return last

        def export(v, g, aT):
            return V.tensor_copy(bexp[:, ds(g.at(2 * U), 2 * U)].rearrange("c (r u) -> c r u", r=2),
                                 aT[:, :, 0:P:P - 1].rearrange("c u r -> c r u"))

        a_ = {k: sem(f"gat_{k}") for k in (
            "dst_rows", "boundary", "own", "same", "far", "dots", "logit", "leaky", "logits", "logit_rows", "max",
            "arg", "weights", "sums", "total", "inverse", "alpha", "matrix", "diagonal", "aggregate", "columns",
            "product", "tanh", "half", "rows", "exported", "lookup", "sum")}

        def gat_pass(l):
            base = GE * l
            kinds = ["es", "gi", "xs", "b2", "fm", "zz", "dd", "ev", "ml", "arg", "w", "rl", "al", "xd", "S", "far",
                     "D", "aT", "xh", "th", "xn"]
            kinds += ["li"] if l == 0 else []
            kinds += ["xr", "xo"] if l == LAYERS - 1 else []
            with ExitStack() as c2:
                t = tiles_of(c2, f"g{l}", kinds)
                junk = sb(f"g{l}_junk", [P, 4 * U, P], f32, c2)
                final = "xo" if l == LAYERS - 1 else "xn"
                done = a_["sum"] if l == LAYERS - 1 else a_["rows"]
                since = base if l == LAYERS - 1 else 0

                def count_done(g, more=1):
                    return g.count(more - (base if l == LAYERS - 1 else 0))

                with nc.Block() as block:
                    @block.sync
                    def _(sp):
                        def load(g):
                            after(sp, a_["rows"], g, UE)
                            if l == LAYERS - 1 and (g.i is not None or g.c - base >= UE):
                                settle(sp)
                                sp.wait_ge(done, count_done(g, 1 - UE))
                            settle(sp)
                            load_group(sp, g, l, t)
                            if l == LAYERS - 1:
                                sp.dma_start(t["xr"][g.slot][:, :, :], slot_rows(raw_rows, g)).then_inc(e_ex[g.slot], 16)

                        def store(g):
                            b = g.slot
                            sp.wait_ge(a_["total"], g.count())
                            settle(sp)
                            sp.dma_start(bstats[:, ds(g.at(2 * U), 2 * U)].rearrange("k (r u) -> r k u", r=2),
                                         t["ml"][b][0:P:P - 1, :, :]).then_inc(e_bs[b], 16)
                            if l == 0:
                                sp.wait_ge(a_["lookup"], g.count())
                                settle(sp)
                                sp.dma_start(lookups[ds(g.at(1), 1), :, :].rearrange("a p u -> (a p) u"),
                                             t["li"][b][:, :]).then_inc(e_lk[b], 16)
                            sp.wait_ge(done, count_done(g))
                            to = mid_rows if l == LAYERS - 1 else tables[l + 1]
                            settle(sp)
                            sp.dma_start(slot_rows(to, g), t[final][b][:, :, :]).then_inc(e_st[b], 16)
                        pipeline(sp, GE, [(0, load), (3, store)], UE, base)
                        for k in range(UE):
                            end = Turn(None, base + GE - UE + (k - (base + GE - UE)) % UE, UE, base)
                            sp.wait_ge(e_bs[k], end.uses())
                            sp.wait_ge(e_st[k], end.uses())
                            if l == 0:
                                sp.wait_ge(e_lk[k], end.uses())

                    @block.gpsimd
                    def _(q):
                        pipeline(q, GE, [(0, lambda g: gather_group(q, g, l, t))], UE, base)

                    @block.tensor
                    def _(pe):
                        def aggregate(g):
                            b = g.slot
                            pe.wait_ge(a_["matrix"], g.count())
                            pe.wait_ge(a_["diagonal"], g.count())
                            after(pe, a_["columns"], g)
                            for u in range(U):
                                T.matmul(banks[4][:, u, :], lhsT=t["xs"][b][:, u, 0:C], rhs=t["S"][b][:, u, :],
                                         start=True, stop=False)
                                last = T.matmul(banks[4][:, u, :], lhsT=t["xd"][b][:, u, :], rhs=t["D"][b][:, u, :],
                                                start=False, stop=True)
                            last.then_inc(a_["aggregate"], 1)

                        def logit_rows(g):
                            pe.wait_ge(a_["logits"], g.count())
                            after(pe, a_["max"], g)
                            for u in range(U):
                                last = T.transpose(banks[2][:, u, :], t["ev"][g.slot][:, 0, u:u + 1].broadcast_to([P, P]),
                                                   ident[:, :])
                            last.then_inc(a_["logit_rows"], 1)

                        def enter(g):
                            pe.wait_ge(e_es[g.slot], g.uses())
                            after(pe, a_["same"], g)
                            tile_matrix_rows(pe, g, t).then_inc(a_["dst_rows"], 1)
                            pe.wait_ge(e_xd[g.slot], g.uses(1, 48))
                            after(pe, a_["own"], g)
                            boundary_values(pe, g, t).then_inc(a_["boundary"], 1)

                        def sums(g):
                            b = g.slot
                            pe.wait_ge(a_["weights"], g.count())
                            after(pe, a_["total"], g)
                            for u in range(U):
                                last = T.matmul(banks[3][:, 0, u:u + 1], lhsT=t["S"][b][:, u, :],
                                                rhs=t["w"][b][:, 0, u:u + 1], start=True, stop=True)
                            last.then_inc(a_["sums"], 1)

                        def product(g):
                            b = g.slot
                            pe.wait_ge(a_["columns"], g.count())
                            after(pe, a_["tanh"], g)
                            T.matmul(banks[5][:, :, :], lhsT=ones3[:, :], rhs=brow3[l][:, :, :], start=True, stop=False,
                                     skip_group_check=True)
                            for u in range(U):
                                last = T.matmul(banks[5][:, u, :], lhsT=t["aT"][b][:, u, :], rhs=gat_w[:, l, :],
                                                start=False, stop=True, skip_group_check=True)
                            last.then_inc(a_["product"], 1)
                        pipeline(pe, GE, [(2, aggregate), (1, logit_rows), (0, enter), (1, sums), (2, product)], UE, base)

                    @block.scalar
                    def _(a):
                        def columns(g):
                            a.wait_ge(a_["aggregate"], g.count())
                            after(a, a_["exported"], g, UE)
                            S.activation(t["aT"][g.slot][:, :, :], banks[4][:, :, :], ACT.Copy).then_inc(a_["columns"], 1)

                        def weights(g):
                            a.wait_ge(a_["arg"], g.count())
                            S.activation(t["w"][g.slot][:, :, :], t["arg"][g.slot][:, :, :], ACT.Exp)\
                             .then_inc(a_["weights"], 1)

                        def half(g):
                            a.wait_ge(a_["own"], g.count())
                            S.activation(t["xh"][g.slot][:, :, :], t["xd"][g.slot][:, :, :], ACT.Copy, bias=0.5)\
                             .then_inc(a_["half"], 1)

                        def tanh(g):
                            a.wait_ge(a_["product"], g.count())
                            S.activation(t["th"][g.slot][:, :, :], banks[5][:, :, :], ACT.Tanh, scale=0.5)\
                             .then_inc(a_["tanh"], 1)

                        def diagonal(g):
                            a.wait_ge(a_["alpha"], g.count())
                            for u in range(U):
                                last = S.activation(t["D"][g.slot][:, u, :], ident[:, :], ACT.Copy,
                                                    scale=t["al"][g.slot][:, 1, u:u + 1])
                            last.then_inc(a_["diagonal"], 1)
                        pipeline(a, GE, [(2, columns), (1, weights), (0, half), (2, tanh), (1, diagonal)], UE, base)

                    @block.vector
                    def _(v):
                        def maxima(g):
                            b = g.slot
                            v.wait_ge(a_["far"], g.count())
                            after_dma(v, e_bs[b], g)
                            v.wait_ge(a_["logit_rows"], g.count())
                            settle(v)
                            for u in range(U):
                                last = V.tensor_tensor_reduce(
                                    out=junk[:, 3 * U + u, :], in0=banks[2][:, u, :], in1=t["far"][b][:, u, :], scale=1.0,
                                    scalar=t["ev"][b][:, 1, u:u + 1], op0=ALU.add, op1=ALU.max,
                                    accum_out=t["ml"][b][:, 0, u:u + 1])
                            last.then_inc(a_["max"], 1)
                            v.wait_ge(a_["max"], g.count())
                            V.tensor_tensor(t["arg"][b][:, :, :], t["ev"][b][:, :, :],
                                            t["ml"][b][:, 0:1, :].broadcast_to([P, 2, U]), ALU.subtract)\
                             .then_inc(a_["arg"], 1)

                        def enter(g):
                            b = g.slot
                            v.wait_ge(e_es[b], g.uses())
                            v.wait_ge(a_["boundary"], g.count())
                            put_boundary_values(v, g, t).then_inc(a_["own"], 1)
                            v.wait_ge(a_["dst_rows"], g.count())
                            V.tensor_tensor(t["S"][b][:, :, :], banks[0][:, :, :], bc(t["es"][b][:, :, DST]),
                                            ALU.is_equal).then_inc(a_["same"], 1)
                            v.wait_ge(e_gx[b], g.uses(1, 16 * U))
                            if l == 0:
                                after_dma(v, e_lk[b], g)
                                V.tensor_copy(t["li"][b][:, :], t["xs"][b][:, :, C]).then_inc(a_["lookup"], 1)
                            v.wait_ge(a_["own"], g.count())
                            for u in range(U):
                                for k, (row, vec, to) in enumerate((
                                        (t["xs"], v_src, t["zz"][b][:, 0, u:u + 1]),
                                        (t["xd"], v_sum, t["zz"][b][:, 1, u:u + 1]),
                                        (t["xd"], v_dst, t["dd"][b][:, u:u + 1]))):
                                    last = V.tensor_tensor_reduce(
                                        out=junk[:, k * U + u, :], in0=row[b][:, u, 0:C], in1=vec[:, l, :], scale=1.0,
                                        scalar=0.0, op0=ALU.mult, op1=ALU.add, accum_out=to)
                            last.then_inc(a_["dots"], 1)
                            v.wait_ge(a_["same"], g.count())
                            V.tensor_scalar(t["far"][b][:, :, :], t["S"][b][:, :, :], FAR, -FAR, ALU.mult, ALU.add)\
                             .then_inc(a_["far"], 1)
                            v.wait_ge(a_["dots"], g.count())
                            V.tensor_tensor(t["zz"][b][:, 0, :], t["zz"][b][:, 0, :], t["dd"][b][:, :], ALU.add)\
                             .then_inc(a_["logit"], 1)
                            v.wait_ge(a_["logit"], g.count())
                            V.scalar_tensor_tensor(out=t["ev"][b][:, :, :], in0=t["zz"][b][:, :, :], scalar=SLOPE,
                                                   in1=t["zz"][b][:, :, :], op0=ALU.mult, op1=ALU.max)\
                             .then_inc(a_["leaky"], 1)
                            v.wait_ge(a_["leaky"], g.count())
                            V.tensor_tensor(t["ev"][b][:, 1, :], t["ev"][b][:, 1, :], t["es"][b][:, :, CARRIED],
                                            ALU.add).then_inc(a_["logits"], 1)

                        def alpha(g):
                            b = g.slot
                            v.wait_ge(a_["sums"], g.count())
                            V.tensor_tensor(t["ml"][b][:, 1, :], banks[3][:, 0, 0:U], t["w"][b][:, 1, :], ALU.add)\
                             .then_inc(a_["total"], 1)
                            v.wait_ge(a_["total"], g.count())
                            V.reciprocal(t["rl"][b][:, :], t["ml"][b][:, 1, :]).then_inc(a_["inverse"], 1)
                            v.wait_ge(a_["inverse"], g.count())
                            V.tensor_tensor(t["al"][b][:, :, :], t["w"][b][:, :, :],
                                            t["rl"][b][:, :].unsqueeze(1).broadcast_to([P, 2, U]), ALU.mult)\
                             .then_inc(a_["alpha"], 1)
                            v.wait_ge(a_["alpha"], g.count())
                            V.tensor_tensor(t["S"][b][:, :, :], t["S"][b][:, :, :], bc(t["al"][b][:, 0, :]), ALU.mult)\
                             .then_inc(a_["matrix"], 1)

                        def leave(g):
                            b = g.slot
                            v.wait_ge(a_["columns"], g.count())
                            export(v, g, t["aT"][b]).then_inc(a_["exported"], 1)
                            after_dma(v, e_st[b], g)
                            v.wait_ge(a_["half"], g.count())
                            v.wait_ge(a_["tanh"], g.count())
                            V.scalar_tensor_tensor(out=t["xn"][b][:, :, :], in0=t["th"][b][:, :, :], scalar=0.5,
                                                   in1=t["xh"][b][:, :, :], op0=ALU.mult, op1=ALU.add)\
                             .then_inc(a_["rows"], 1)
                            if l == LAYERS - 1:
                                v.wait_ge(e_ex[b], g.uses(since=base))
                                v.wait_ge(a_["rows"], g.count())
                                V.tensor_tensor(t["xo"][b][:, :, :], t["xn"][b][:, :, :], t["xr"][b][:, :, :], ALU.add)\
                                 .then_inc(a_["sum"], 1)
                        pipeline(v, GE, [(1, maxima), (0, enter), (1, alpha), (2, leave)], UE, base)

        n_ = {k: sem(f"net_{k}") for k in (
            "dst_rows", "boundary", "own", "matrix", "src_t", "src_c", "own_t", "own_c", "edge", "edge_relu",
            "edge_t", "edge_c", "aggregate", "columns", "node", "rows", "exported", "sum")}
        n_ea, n_es, n_sc = sems("n_edge_feats_loaded"), sems("n_edge_feats_stored"), sems("n_scattered")

        def net_pass(l):
            L = LAYERS + l
            base = GE * L
            nbase = GE * LAYERS
            last_layer = l == LAYERS - 1
            kinds = ["es", "gi", "xs", "xd", "b2", "fm", "A", "sT", "dT", "eT", "eR", "aT", "xn"]
            kinds += ["ea"] if l else []
            kinds += ["xm", "xo"] if last_layer else []

            def cnt(g, more=1):
                return g.count(more - nbase)

            def aft(eng, s, g, back=1):
                if g.i is not None or g.c - nbase >= back:
                    eng.wait_ge(s, cnt(g, 1 - back))

            with ExitStack() as c2:
                t = tiles_of(c2, f"n{l}", kinds)
                with nc.Block() as block:
                    @block.sync
                    def _(sp):
                        def load(g):
                            b = g.slot
                            aft(sp, n_["rows"], g, UE)
                            if last_layer:
                                settle(sp)
                                after_dma(sp, n_sc[b], g, 16 * U, base)
                            settle(sp)
                            load_group(sp, g, L, t)
                            if l:
                                sp.dma_start(t["ea"][b][:, :, :], edge_feats[ds(g.at(1), 1), :, :].rearrange(
                                    "a c (u e) -> (a c) u e", u=U)).then_inc(n_ea[b], 16)
                            if last_layer:
                                sp.dma_start(t["xm"][b][:, :, :], slot_rows(mid_rows, g)).then_inc(e_ex[b], 16)

                        def store(g):
                            b = g.slot
                            if not last_layer:
                                sp.wait_ge(n_["edge_relu"], cnt(g))
                                settle(sp)
                                sp.dma_start(edge_feats[ds(g.at(1), 1), :, :].rearrange("a c (u e) -> (a c) u e", u=U),
                                             t["eT"][b][:, :, :]).then_inc(n_es[b], 16)
                                sp.wait_ge(n_["rows"], cnt(g))
                                settle(sp)
                                sp.dma_start(slot_rows(tables[L + 1], g), t["xn"][b][:, :, :]).then_inc(e_st[b], 16)
                        pipeline(sp, GE, [(0, load), (3, store)], UE, base)
                        if not last_layer:
                            for k in range(UE):
                                end = Turn(None, base + GE - UE + (k - (base + GE - UE)) % UE, UE, base)
                                sp.wait_ge(e_st[k], end.uses())
                                sp.wait_ge(n_es[k], end.uses(since=nbase))

                    @block.gpsimd
                    def _(q):
                        def scatter(g):
                            b = g.slot
                            q.wait_ge(n_["sum"], cnt(g, 1 - GE * l))
                            settle(q)
                            for u in range(U):
                                q.indirect_dma_start(
                                    out=out, out_offset=bass.IndirectOffsetOnAxis(
                                        ap=t["es"][b][:, u, OUTI:OUTI + 1].bitcast(i32), axis=0),
                                    in_=t["xo"][b][:, u, :], in_offset=None,
                                    bounds_check=N - 1, oob_is_err=False).then_inc(n_sc[b], 16)
                        work = [(0, lambda g: gather_group(q, g, L, t))]
                        pipeline(q, GE, work + ([(3, scatter)] if last_layer else []), UE, base)
                        if last_layer:
                            for k in range(UE):
                                end = Turn(None, base + GE - UE + (k - (base + GE - UE)) % UE, UE, base)
                                q.wait_ge(n_sc[k], end.uses(1, 16 * U, since=base))

                    @block.tensor
                    def _(pe):
                        def aggregate(g):
                            b = g.slot
                            pe.wait_ge(n_["edge_c"], cnt(g))
                            pe.wait_ge(n_["matrix"], cnt(g))
                            aft(pe, n_["columns"], g)
                            for u in range(U):
                                last = T.matmul(banks[6][:, u, :], lhsT=t["eR"][b][:, u, :], rhs=t["A"][b][:, u, :],
                                                start=True, stop=True)
                            last.then_inc(n_["aggregate"], 1)

                        def edge(g):
                            b = g.slot
                            pe.wait_ge(n_["src_c"], cnt(g))
                            pe.wait_ge(n_["own_c"], cnt(g))
                            if l:
                                pe.wait_ge(n_ea[b], g.uses(since=base - GE * (l - 1)))
                            aft(pe, n_["edge_relu"], g)
                            parts = [t["sT"], t["dT"]] + ([t["ea"]] if l else [])
                            for k, part in enumerate(parts):
                                last = T.matmul(banks[4][:, :, :], lhsT=we[l][:, k, :], rhs=part[b][:, :, :],
                                                start=k == 0, stop=k == len(parts) - 1)
                            last.then_inc(n_["edge"], 1)

                        def enter(g):
                            b = g.slot
                            pe.wait_ge(e_es[b], g.uses())
                            aft(pe, n_["matrix"], g)
                            tile_matrix_rows(pe, g, t).then_inc(n_["dst_rows"], 1)
                            pe.wait_ge(e_xd[b], g.uses(1, 48))
                            aft(pe, n_["own"], g)
                            boundary_values(pe, g, t).then_inc(n_["boundary"], 1)
                            pe.wait_ge(e_gx[b], g.uses(1, 16 * U))
                            aft(pe, n_["src_c"], g)
                            for u in range(U):
                                last = T.transpose(banks[2][:, u, :], t["xs"][b][:, u, 0:C], ident[:, :])
                            last.then_inc(n_["src_t"], 1)

                        def edge_rows(g):
                            pe.wait_ge(n_["edge_relu"], cnt(g))
                            aft(pe, n_["edge_c"], g)
                            for u in range(U):
                                last = T.transpose(banks[5][:, u, :], t["eT"][g.slot][:, u, :], ident[:, :])
                            last.then_inc(n_["edge_t"], 1)

                        def node(g):
                            b = g.slot
                            pe.wait_ge(n_["columns"], cnt(g))
                            aft(pe, n_["rows"], g)
                            T.matmul(banks[7][:, :, :], lhsT=ones3[:, :], rhs=brow3[L][:, :, :], start=True, stop=False,
                                     skip_group_check=True)
                            for u in range(U):
                                T.matmul(banks[7][:, u, :], lhsT=t["dT"][b][:, u, :], rhs=wn[l][:, 0, :],
                                         start=False, stop=False, skip_group_check=True)
                                last = T.matmul(banks[7][:, u, :], lhsT=t["aT"][b][:, u, :], rhs=wn[l][:, 1, :],
                                                start=False, stop=True, skip_group_check=True)
                            last.then_inc(n_["node"], 1)

                        def own_columns(g):
                            pe.wait_ge(n_["own"], cnt(g))
                            aft(pe, n_["own_c"], g)
                            for u in range(U):
                                last = T.transpose(banks[3][:, u, :], t["xd"][g.slot][:, u, :], ident[:, :])
                            last.then_inc(n_["own_t"], 1)
                        pipeline(pe, GE, [(2, aggregate), (1, edge), (0, enter), (1, edge_rows), (2, node),
                                          (0, own_columns)], UE, base)

                    @block.scalar
                    def _(a):
                        def columns(g):
                            a.wait_ge(n_["aggregate"], cnt(g))
                            aft(a, n_["exported"], g, UE)
                            S.activation(t["aT"][g.slot][:, :, :], banks[6][:, :, :], ACT.Copy).then_inc(n_["columns"], 1)

                        def edge_relu(g):
                            if not last_layer:
                                after_dma(a, n_es[g.slot], g, 16, nbase)
                            a.wait_ge(n_["edge"], cnt(g))
                            S.activation(t["eT"][g.slot][:, :, :], banks[4][:, :, :], ACT.Relu,
                                         bias=edge_b[:, l:l + 1]).then_inc(n_["edge_relu"], 1)

                        def src_columns(g):
                            a.wait_ge(n_["src_t"], cnt(g))
                            S.activation(t["sT"][g.slot][:, :, :], banks[2][:, :, :], ACT.Copy).then_inc(n_["src_c"], 1)

                        def rows(g):
                            if last_layer:
                                aft_last(a, g)
                            else:
                                after_dma(a, e_st[g.slot], g)
                            a.wait_ge(n_["node"], cnt(g))
                            S.activation(t["xn"][g.slot][:, :, :], banks[7][:, :, :], ACT.Relu).then_inc(n_["rows"], 1)

                        def aft_last(a, g):
                            if g.i is not None or g.c - base >= UE:
                                a.wait_ge(n_["sum"], cnt(g, 1 - UE - GE * l))
                        pipeline(a, GE, [(2, columns), (1, edge_relu), (0, src_columns), (2, rows)], UE, base)

                    @block.vector
                    def _(v):
                        def enter(g):
                            b = g.slot
                            v.wait_ge(e_es[b], g.uses())
                            v.wait_ge(n_["dst_rows"], cnt(g))
                            for u in range(U):
                                last = V.tensor_scalar(t["A"][b][:, u, :], banks[0][:, u, :],
                                                       t["es"][b][:, u, DST:DST + 1], t["es"][b][:, u, NORM:NORM + 1],
                                                       ALU.is_equal, ALU.mult)
                            last.then_inc(n_["matrix"], 1)
                            v.wait_ge(n_["boundary"], cnt(g))
                            put_boundary_values(v, g, t).then_inc(n_["own"], 1)

                        def edge_copy(g):
                            v.wait_ge(n_["edge_t"], cnt(g))
                            V.tensor_copy(t["eR"][g.slot][:, :, :], banks[5][:, :, :]).then_inc(n_["edge_c"], 1)

                        def leave(g):
                            b = g.slot
                            v.wait_ge(n_["columns"], cnt(g))
                            export(v, g, t["aT"][b]).then_inc(n_["exported"], 1)

                        def own_copy(g):
                            v.wait_ge(n_["own_t"], cnt(g))
                            V.tensor_copy(t["dT"][g.slot][:, :, :], banks[3][:, :, :]).then_inc(n_["own_c"], 1)

                        def add(g):
                            b = g.slot
                            after_dma(v, n_sc[b], g, 16 * U, base)
                            v.wait_ge(e_ex[b], g.uses(since=base, before=uses_before(GE * (LAYERS - 1), b)))
                            v.wait_ge(n_["rows"], cnt(g))
                            V.tensor_tensor(t["xo"][b][:, :, :], t["xn"][b][:, :, :], t["xm"][b][:, :, :], ALU.add)\
                             .then_inc(n_["sum"], 1)
                        pipeline(v, GE, [(0, enter), (1, edge_copy), (2, leave), (0, own_copy)]
                                 + ([(2, add)] if last_layer else []), UE, base)

        b_ = {k: sem(f"bnd_{k}") for k in ("loaded", "rows", "scaled", "max", "exp", "scale", "total", "inv",
                                            "sum", "sum_t", "sum_c", "out", "act", "half", "new", "stored", "scattered", "own_t",
                                            "own_c", "mid")}
        b_count = dict.fromkeys(b_, 0)

        def boundary_pass(L):
            gat = L < LAYERS
            l = L % LAYERS
            ends = L == 2 * LAYERS - 1
            W = C + 1 if gat else C

            def halves(k0, j):
                return banks[k0 + j // 4], j % 4

            at = dict(b_count)

            def up(k, n=1):
                b_count[k] += n
                return b_count[k]

            with ExitStack() as c2:
                xb = sb(f"b{L}_x", [BP, BJ, C], f32, c2)
                ex = sb(f"b{L}_ex", [BP, BJ, W], f32, c2)
                tot = sb(f"b{L}_tot", [BP, BJ, C], f32, c2)
                totT = sb(f"b{L}_totT", [C, BJ, BP], f32, c2)
                ownT = sb(f"b{L}_ownT", [C, BJ, BP], f32, c2)
                act = sb(f"b{L}_act", [BP, BJ, C], f32, c2)
                new = sb(f"b{L}_new", [BP, BJ, C], f32, c2)
                nrm = sb(f"b{L}_nrm", [BP, BJ, C], f32, c2)
                junk = sb(f"b{L}_junk", [BP, BJ if gat else 1, NB], f32, c2)
                mrow = sb(f"b{L}_mrow", [BP, NB], f32, c2)
                sc = sb(f"b{L}_sc", [BP, 6, BJ], f32, c2)
                tn = norm_tiles(c2, f"b{L}", 1, BJ)[0]
                zn = norm_sems(f"b{L}_norm") if L == LAYERS - 1 else None
                loads = [(xb[:, :, :], boundary_rows(own_of(L), EP))]
                if gat:
                    loads += [(sc[:, 0:2, :], bstats.rearrange("k (j p) -> p k j", p=BP)),
                              (mrow[:, :], bstats[0:1, :].broadcast_to([BP, NB]))]
                n_load = up("loaded", 16 * len(loads))
                v_rows, v_scaled = up("rows"), up("scaled")
                with nc.Block() as block:
                    @block.sync
                    def _(sp):
                        with nc.allow_non_contiguous_dma("statistics by partition"):
                            for to, of in loads:
                                sp.dma_start(to, of).then_inc(b_["loaded"], 16)
                        if not ends:
                            if L == LAYERS - 1:
                                sp.wait_ge(zn["done"], 1)
                                settle(sp)
                                sp.dma_start(boundary_rows(tables[L + 1], EP), nrm[:, :, :]).then_inc(b_["stored"], 16)
                            else:
                                sp.wait_ge(b_["new"], at["new"] + 1)
                                settle(sp)
                                sp.dma_start(boundary_rows(tables[L + 1], EP), new[:, :, :]).then_inc(b_["stored"], 16)
                            sp.wait_ge(b_["stored"], at["stored"] + 16)

                    @block.gpsimd
                    def _(q):
                        if ends:
                            q.wait_ge(b_["new"], at["new"] + 1)
                            for j in range(BJ):
                                q.indirect_dma_start(
                                    out=out, out_offset=bass.IndirectOffsetOnAxis(ap=bout[:, j:j + 1], axis=0),
                                    in_=new[:, j, :], in_offset=None,
                                    bounds_check=N - 1, oob_is_err=False).then_inc(b_["scattered"], 16)
                            q.wait_ge(b_["scattered"], 16 * BJ)

                    @block.tensor
                    def _(pe):
                        for j in range(BJ):
                            bank, k = halves(0, j)
                            last = T.transpose(bank[0:BP, k, :], bexp[:, j * BP:(j + 1) * BP], ident[:, :])
                        last.then_inc(b_["rows"], 1)
                        pe.wait_ge(b_["scaled"], v_scaled)
                        for j in range(BJ):
                            to = flat_banks[2 + j // 3][0:BP, (j % 3) * W:(j % 3 + 1) * W]
                            for k in range(BJ):
                                last = T.matmul(to, lhsT=same[:, k, j * BP:(j + 1) * BP], rhs=ex[:, k, :],
                                                start=k == 0, stop=k == BJ - 1)
                        last.then_inc(b_["total"], 1)
                        if not gat:
                            pe.wait_ge(b_["loaded"], n_load)
                            for j in range(BJ):
                                bank, k = halves(0, j)
                                last = T.transpose(bank[:, k, 0:BP], xb[:, j, :], ident[0:BP, 0:BP])
                            last.then_inc(b_["own_t"], 1)
                        pe.wait_ge(b_["sum"], at["sum"] + 1)
                        for j in range(BJ):
                            bank, k = halves(5, j)
                            last = T.transpose(bank[:, k, 0:BP], tot[:, j, :], ident[0:BP, 0:BP])
                        last.then_inc(b_["sum_t"], 1)
                        pe.wait_ge(b_["sum_c"], at["sum_c"] + 1)
                        if not gat:
                            pe.wait_ge(b_["own_c"], at["own_c"] + 1)
                        for h, m in ((0, 4), (1, BJ - 4)):
                            T.matmul(banks[2 + h][0:BP, 0:m, :], lhsT=ones3[:, 0:BP], rhs=brow3[L][:, 0:m, :],
                                     start=True, stop=False, skip_group_check=True)
                            for k in range(m):
                                j = 4 * h + k
                                to = banks[2 + h][0:BP, k, :]
                                if not gat:
                                    T.matmul(to, lhsT=ownT[:, j, :], rhs=wn[l][:, 0, :], start=False, stop=False,
                                             skip_group_check=True)
                                last = T.matmul(to, lhsT=totT[:, j, :], rhs=gat_w[:, l, :] if gat else wn[l][:, 1, :],
                                                start=False, stop=True, skip_group_check=True)
                        last.then_inc(b_["out"], 1)

                    @block.scalar
                    def _(a):
                        if gat:
                            a.wait_ge(b_["max"], at["max"] + 2)
                            S.activation(sc[:, 3, :], sc[:, 4, :], ACT.Exp).then_inc(b_["exp"], 1)
                            a.wait_ge(b_["loaded"], n_load)
                            S.activation(xb[:, :, :], xb[:, :, :], ACT.Copy, bias=0.5).then_inc(b_["half"], 1)
                        a.wait_ge(b_["sum_t"], at["sum_t"] + 1)
                        for h, m in ((0, 4), (1, BJ - 4)):
                            last = S.activation(totT[:, 4 * h:4 * h + m, :], banks[5 + h][:, 0:m, 0:BP], ACT.Copy)
                        last.then_inc(b_["sum_c"], 1)
                        a.wait_ge(b_["out"], at["out"] + 1)
                        for h, m in ((0, 4), (1, BJ - 4)):
                            last = S.activation(act[:, 4 * h:4 * h + m, :], banks[2 + h][0:BP, 0:m, :],
                                                ACT.Tanh if gat else ACT.Relu, scale=0.5 if gat else 1.0)
                        last.then_inc(b_["act"], 1)
                        if zn:
                            norm_scalar_a(a, zn, tn, 1, BP, BJ)
                            norm_scalar_b(a, zn, tn, braw, nrm, 1, BP, BJ)

                    @block.vector
                    def _(v):
                        if gat:
                            v.wait_ge(b_["loaded"], n_load)
                            for j in range(BJ):
                                last = V.tensor_tensor_reduce(out=junk[:, j, :], in0=mrow[:, :], in1=far[:, j, :], scale=1.0,
                                                              scalar=-FAR, op0=ALU.add, op1=ALU.max,
                                                              accum_out=sc[:, 2, j:j + 1])
                            last.then_inc(b_["max"], 1)
                            v.wait_ge(b_["max"], at["max"] + 1)
                            V.tensor_tensor(sc[:, 4, :], sc[:, 0, :], sc[:, 2, :], ALU.subtract).then_inc(b_["max"], 1)
                            v.wait_ge(b_["exp"], at["exp"] + 1)
                            V.tensor_tensor(sc[:, 5, :], sc[:, 3, :], sc[:, 1, :], ALU.mult).then_inc(b_["scale"], 1)
                            v.wait_ge(b_["scale"], at["scale"] + 1)
                        v.wait_ge(b_["rows"], v_rows)
                        for h, m in ((0, 4), (1, BJ - 4)):
                            to, of = ex[:, 4 * h:4 * h + m, 0:C], banks[h][0:BP, 0:m, :]
                            if gat:
                                last = V.tensor_tensor(to, of, sc[:, 5, 4 * h:4 * h + m].unsqueeze(2)
                                                       .broadcast_to([BP, m, C]), ALU.mult)
                            else:
                                last = V.tensor_copy(to, of)
                        if gat:
                            last = V.tensor_copy(ex[:, :, C], sc[:, 5, :])
                        last.then_inc(b_["scaled"], 1)
                        v.wait_ge(b_["total"], at["total"] + 1)
                        sums = [(flat_banks[2 + h][0:BP, 0:m * W].rearrange("p (j w) -> p j w", w=W), 3 * h, m)
                                for h, m in ((0, 3), (1, 3), (2, BJ - 6))]
                        if gat:
                            for of, j, m in sums:
                                last = V.reciprocal(sc[:, 4, j:j + m], of[:, :, C])
                            last.then_inc(b_["inv"], 1)
                            v.wait_ge(b_["inv"], at["inv"] + 1)
                        for of, j, m in sums:
                            if gat:
                                last = V.tensor_tensor(tot[:, j:j + m, :], of[:, :, 0:C],
                                                       sc[:, 4, j:j + m].unsqueeze(2).broadcast_to([BP, m, C]), ALU.mult)
                            else:
                                last = V.tensor_copy(tot[:, j:j + m, :], of[:, :, 0:C])
                        last.then_inc(b_["sum"], 1)
                        if not gat:
                            v.wait_ge(b_["own_t"], at["own_t"] + 1)
                            for h, m in ((0, 4), (1, BJ - 4)):
                                last = V.tensor_copy(ownT[:, 4 * h:4 * h + m, :], banks[h][:, 0:m, 0:BP])
                            last.then_inc(b_["own_c"], 1)
                        v.wait_ge(b_["act"], at["act"] + 1)
                        if gat:
                            v.wait_ge(b_["half"], at["half"] + 1)
                            last = V.scalar_tensor_tensor(out=new[:, :, :], in0=act[:, :, :], scalar=0.5, in1=xb[:, :, :],
                                                          op0=ALU.mult, op1=ALU.add)
                        elif ends:
                            last = V.tensor_tensor(new[:, :, :], act[:, :, :], braw[:, :, :], ALU.add)
                        else:
                            last = V.tensor_copy(new[:, :, :], act[:, :, :])
                        last.then_inc(b_["new"], 1)
                        if zn:
                            v.wait_ge(b_["new"], at["new"] + 1)
                            V.tensor_tensor(braw[:, :, :], braw[:, :, :], new[:, :, :], ALU.add).then_inc(b_["mid"], 1)
                            v.wait_ge(b_["mid"], 1)
                            norm_vector_a(v, zn, tn, braw, 1, BP, BJ)
                            norm_vector_b(v, zn, tn, 1, BP, BJ)
            for k in ("max",):
                b_count[k] += 2 * gat
            for k in ("exp", "half", "scale", "inv"):
                b_count[k] += gat
            for k in ("own_t", "own_c"):
                b_count[k] += not gat
            for k in ("total", "sum", "sum_t", "sum_c", "out", "act", "new"):
                b_count[k] += 1
            b_count["stored"] += 16

        for l in range(LAYERS):
            gat_pass(l)
            boundary_pass(l)
        norm_pass("mid_norm", GE, lambda g: slot_rows(mid_rows, g), lambda g: slot_rows(tables[LAYERS], g), C, 4, 0)
        for l in range(LAYERS):
            net_pass(l)
            boundary_pass(LAYERS + l)
        end_phase()


_RUNS = "x edges edge_w dst_rows src_lookups bnd_rows bnd_cols bnd_numbers slot_numbers node_numbers tail_numbers " \
        "eye gat_w gat_wt att gat_b node_b edge_b bias_rows We0 Wn0 We1 Wn1 We2 Wn2".split()


def laid_out(i):
    def padded(a, fill):
        return np.concatenate([a, np.full(EP - E, fill, a.dtype)])

    src, dst = padded(np.asarray(i["src"]), 0), padded(np.asarray(i["dst"]), N)
    tiles = dst.reshape(-1, P)
    first, last = tiles[:, 0], tiles[:, -1]
    before = np.concatenate([np.full(1, -1, dst.dtype), last[:-1]])
    behind = np.concatenate([first[1:], np.full(1, N, dst.dtype)])

    def columns(a):
        return np.broadcast_to(a.reshape(len(tiles), -1), tiles.shape).T

    def bounds(a, b):
        return np.stack([a.reshape(GE, U), b.reshape(GE, U)], 1).reshape(NB)

    edges = np.stack([columns(a) for a in (dst, src, np.concatenate([dst[1:], behind[-1:]]), first, last, before)], 1)
    bnd = bounds(first, last)
    bnd_cols = np.stack([a.reshape(BJ, BP).T for a in (bnd, bounds(np.full_like(first, -1), first),
                                                       bounds(last, behind))], 1)
    slot = np.arange(EP).reshape(GE, P, U).transpose(1, 0, 2).reshape(P, GE * U)
    ws = np.asarray(i["L0_gnn_Ws"])
    gb = np.asarray(i["L0_gnn_bias"])
    nb = np.stack([np.asarray(i[f"L1_gnn_bn{l}"]) for l in range(LAYERS)])
    eb = np.stack([np.asarray(i[f"L1_gnn_be{l}"]) for l in range(LAYERS)])
    arrays = dict(
        x=np.asarray(i["x"]), edges=edges, edge_w=padded(np.asarray(i["edge_weight"]), 0).reshape(-1, P).T,
        dst_rows=dst.reshape(GE, U, P), src_lookups=src.reshape(GE, U, P).transpose(0, 2, 1),
        bnd_rows=bnd.reshape(1, NB), bnd_cols=bnd_cols,
        bnd_numbers=(EP + np.arange(NB)).reshape(BJ, BP).T.astype(np.float32),
        slot_numbers=slot.astype(np.float32),
        node_numbers=(NODE0 + np.arange(P * U)).reshape(P, U).astype(np.float32),
        tail_numbers=(NODE0 + GN * P * U + np.arange(TAIL)).reshape(TP, TU).astype(np.float32),
        eye=np.eye(P, dtype=np.float32), gat_w=ws.transpose(1, 0, 2), gat_wt=ws.transpose(2, 0, 1),
        att=np.concatenate([np.asarray(i["L0_gnn_att_src"]), np.asarray(i["L0_gnn_att_dst"])]).T,
        gat_b=gb.T, node_b=nb.T, edge_b=eb.T,
        bias_rows=np.broadcast_to(np.concatenate([gb, nb]), (3, 2 * LAYERS, C)))
    for l in range(LAYERS):
        arrays[f"We{l}"] = np.asarray(i[f"L1_gnn_We{l}"])
        arrays[f"Wn{l}"] = np.asarray(i[f"L1_gnn_Wn{l}"])
    return {k: np.ascontiguousarray(v) for k, v in arrays.items()}


def kernel(**inputs):
    import concourse.bacc as _bacc
    from concourse import mybir as _mybir
    from concourse.bass_utils import run_bass_kernel_spmd as _run

    nc = _bacc.Bacc("TRN2", target_bir_lowering=False, num_devices=1)
    laid = laid_out(inputs)
    arrays, args = {}, []
    for name in _RUNS:
        a = laid[name]
        arrays[f"in_{name}_dram"] = a
        args.append(nc.dram_tensor(f"in_{name}_dram", a.shape, _mybir.dt.from_np(a.dtype), kind="ExternalInput").ap())
    args.append(nc.dram_tensor("out_0_dram", (N, C), _mybir.dt.from_np(np.dtype("float32")), kind="ExternalOutput").ap())
    build(nc, *args)
    r = _run(nc, [arrays], core_ids=[0])
    return r.results[0]["out_0_dram"]
```

```python
import numpy as np
import concourse.bass as bass
from concourse import mybir
from contextlib import ExitStack

N = 100000
E = 50000
C = 128
P = 128
U = 4
GE = -(-E // (P * U))
EP = GE * P * U
NB = GE * U * 2
BJ = 7
BP = NB // BJ
ROWS = EP + NB + N
NODE0 = EP + NB
W0 = 132
GN = N // (P * U)
TAIL = N - GN * P * U
TP, TU = 80, 2
assert BP * BJ == NB and TP * TU == TAIL and BP <= P
LAYERS = 3
SKIP = 1 << 18
FAR = 1.0e30
EPS = 1e-5
SLOPE = 0.2
NF = 12
(DST, NORM, KEEP, CARRIED, DSTI, OUTI, MAPI), MAPV = range(7), 8
UE = 6
UX = 4


class Turn:

    def __init__(self, i, c, un, base=0):
        self.i, self.c, self.un, self.base = i, c, un, base
        self.slot = c % un

    def value(self, c, per_turn):
        return c if self.i is None else self.i * per_turn + c

    def count(self, more=1):
        return self.value(self.c + more, self.un)

    def uses(self, more=1, each=16, since=0, before=0):
        first = since + (self.slot - since) % self.un
        return self.value(((self.c - first) // self.un + before + more) * each, each)

    def part_uses(self, n, more=1, each=16):
        return self.value((self.c // n + more) * each, self.un // n * each)

    def before(self, back):
        return Turn(self.i, self.c - back, self.un, self.base)

    def at(self, size):
        return self.value((self.c - self.base) * size, self.un * size)


def uses_before(since, slot):
    return len([g for g in range(since, since + GE) if g % UE == slot])


def pipeline(eng, groups, work, un, base=0, last_peeled=0):
    low = min(lag for lag, _ in work)
    work = [(lag - low, fn) for lag, fn in work]
    depth = max(lag for lag, _ in work)
    first = depth + un
    turns = (groups - last_peeled - first) // un

    def step(s, i):
        for lag, fn in work:
            g = s - lag
            if i is not None or 0 <= g < groups:
                fn(Turn(i, g + base, un, base))

    for s in range(first):
        step(s, None)
    with eng.Fori(0, turns) as i:
        for k in range(un):
            step(first + k, i)
    for s in range(first + turns * un, groups + depth):
        step(s, None)


def pipeline_pair(eng, node_work, edge_work):
    def step(s, i):
        for half in range(2):
            for lag, fn in node_work:
                g = 2 * s + half - lag
                if i is not None or 0 <= g <= GN:
                    fn(Turn(i, g, 2 * UX))
            for lag, fn in edge_work[half::2]:
                g = s - lag
                if i is not None or 0 <= g < GE:
                    fn(Turn(i, g, UX))

    depth = max([lag for lag, _ in edge_work] + [-(-lag // 2) for lag, _ in node_work])
    first = depth + UX
    turns = (GN // 2 - first) // UX
    for s in range(first):
        step(s, None)
    with eng.Fori(0, turns) as i:
        for k in range(UX):
            step(first + k, i)
    for s in range(first + turns * UX, GE + depth):
        step(s, None)


def after(eng, sem, g, back=1):
    if g.i is not None or g.c >= back:
        eng.wait_ge(sem, g.count(1 - back))


def after_part(eng, sem, g, n):
    if g.i is not None or g.c >= n:
        eng.wait_ge(sem, g.part_uses(n, 0))


def after_dma(eng, sem, g, each=16, since=0):
    if g.i is not None or g.c - since >= g.un:
        eng.wait_ge(sem, g.uses(0, each, since))


def after_dma_of(eng, sems, g, back, each=16, since=0):
    if g.i is not None or g.c - since >= back:
        old = g.before(back)
        eng.wait_ge(sems[old.slot], old.uses(1, each, since))


class Ring:

    def __init__(self, buffers):
        self.buffers = buffers

    def __getitem__(self, g):
        return self.buffers[g.c % len(self.buffers)]


def build(nc, x, edges, edge_w, dst_rows, src_lookups, bnd_rows, bnd_cols, bnd_numbers, slot_numbers, node_numbers,
          tail_numbers, eye, gat_w_in, gat_wt_in, att_in, gat_b_in, node_b_in, edge_b_in, bias_rows_in,
          We0, Wn0, We1, Wn1, We2, Wn2, out):
    f32, i32, bf16 = mybir.dt.float32, mybir.dt.int32, mybir.dt.bfloat16
    ALU, ACT = mybir.AluOpType, mybir.ActivationFunctionType
    V, S, T, Q = nc.vector, nc.scalar, nc.tensor, nc.gpsimd
    ds = bass.ds
    NT = GE * U

    def dram(name, shape, dt=f32):
        return nc.dram_tensor(name, shape, dt, kind="Internal").ap()

    tables = [dram("table0", [N, W0])] + [dram(f"table{l}", [ROWS, C]) for l in range(1, 2 * LAYERS)]
    own0 = dram("own0", [EP + NB, C])
    raw_rows = dram("raw_rows", [EP, C])
    mid_rows = dram("mid_rows", [EP, C])
    mid_nodes = dram("mid_nodes", [N, C])
    records = dram("records", [GE, P, U * NF])
    lookups = dram("lookups", [GE, P, U], i32)
    bmasks = dram("bmasks", [GE, 2, U * P])
    bstats = dram("bstats", [2, NB])
    edge_feats = dram("edge_feats", [GE, C, U * P])

    with ExitStack() as ctx:
        def sb(name, shape, dt=f32, c=None):
            return (c or ctx).enter_context(nc.sbuf_tensor(name, shape, dt))

        settled = {}
        in_phase = []

        def sem(name):
            in_phase.append(nc.alloc_semaphore(name=name))
            return in_phase[-1]

        def end_phase(done=None):
            done = list(in_phase if done is None else done)
            nc.clear_and_free_semaphores(done)
            in_phase[:] = [s for s in in_phase if not any(s is d for d in done)]
            nc.all_engine_barrier()


        def settle(eng):
            if eng.engine not in settled:
                settled[eng.engine] = nc.alloc_semaphore(name=f"settled_{len(settled)}")
            eng.sem_inc(settled[eng.engine], 1)

        def sems(name, n=4):
            return [sem(f"{name}{k}") for k in range(n)]

        banks = [ctx.enter_context(nc.psum_tensor(f"bank{k}", [P, U, P], f32)) for k in range(8)]
        flat_banks = [b[:, :, :].rearrange("p u e -> p (u e)") for b in banks]

        ident = sb("ident", [P, P])
        ones3 = sb("ones3", [3, P], bf16)
        gat_w = sb("gat_w", [C, LAYERS, C])
        gat_b = sb("gat_b", [C, LAYERS])
        edge_b = sb("edge_b", [C, LAYERS])
        node_b = sb("node_b", [C, LAYERS])
        v_src = sb("v_src", [P, LAYERS, C])
        v_dst = sb("v_dst", [P, LAYERS, C])
        v_sum = sb("v_sum", [P, LAYERS, C])
        we = [sb(f"we{l}", [C, 2 + (l > 0), C]) for l in range(LAYERS)]
        wn = [sb(f"wn{l}", [C, 2, C]) for l in range(LAYERS)]
        brow3 = [sb(f"brow3_{l}", [3, U, C], bf16) for l in range(2 * LAYERS)]
        far = sb("far", [BP, BJ, NB])
        same = sb("same", [BP, BJ, NB])
        bexp = sb("bexp", [C, NB])
        braw = sb("braw", [BP, BJ, C])
        bout = sb("bout", [BP, BJ], i32)
        bclip = sb("bclip", [BP, BJ], i32)
        bmapi = sb("bmapi", [BP, BJ], i32)
        bmapv = sb("bmapv", [BP, BJ, 4])

        s_cl = sem("constants_loaded")
        s_el = sem("edges_loaded")
        s_dv = sem("setup_vector_step")
        s_pe = sem("products_ready")
        s_st = sem("setup_stored")
        with ExitStack() as c1:
            wT = sb("wT", [C, LAYERS, C], f32, c1)
            att = sb("att", [C, 2 * LAYERS], f32, c1)
            bias_rows = sb("bias_rows", [3, 2 * LAYERS, C], f32, c1)
            brest = sb("brest", [3, 2 * LAYERS, C], f32, c1)
            part = [sb(f"bpart{k}", [3, 2 * LAYERS, C], bf16, c1) for k in range(3)]
            edge_i = sb("edge_i", [P, 6, NT], i32, c1)
            edge_f = sb("edge_f", [P, 6, NT], f32, c1)
            wcol = sb("wcol", [P, NT], f32, c1)
            slots = sb("slots", [P, NT], f32, c1)
            tmp = sb("tmp", [P, 5, NT], f32, c1)
            rec = sb("rec", [P, NT, NF], f32, c1)
            row_i = sb("row_i", [GE, U, P], i32, c1)
            row_f = sb("row_f", [GE, U, P], f32, c1)
            row_m = sb("row_m", [GE, 3, U, P], f32, c1)
            brow_i = sb("brow_i", [BP, NB], i32, c1)
            brow_f = sb("brow_f", [BP, NB], f32, c1)
            bcol_i = sb("bcol_i", [BP, 3, BJ], i32, c1)
            bcol = sb("bcol", [BP, 3, BJ], f32, c1)
            btmp = sb("btmp", [BP, 3, BJ], f32, c1)
            f_dst, f_src, f_nxt, f_first, f_last, f_prev = (edge_f[:, k, :] for k in range(6))
            rec_i = rec[:, :, :].bitcast(i32)
            consts = [(ident[:, :], eye), (gat_w[:, :, :], gat_w_in), (wT[:, :, :], gat_wt_in),
                      (att[:, :], att_in), (gat_b[:, :], gat_b_in), (node_b[:, :], node_b_in),
                      (edge_b[:, :], edge_b_in), (bias_rows[:, :, :], bias_rows_in)]
            for l, (a, b) in enumerate(((We0, Wn0), (We1, Wn1), (We2, Wn2))):
                consts += [(we[l][:, :, :], a.rearrange("(k p) c -> p k c", p=C)),
                           (wn[l][:, :, :], b.rearrange("(k p) c -> p k c", p=C))]
            edge_loads = [(edge_i[:, :, :], edges), (wcol[:, :], edge_w), (slots[:, :], slot_numbers),
                          (row_i[:, :, :], dst_rows), (bcol_i[:, :, :], bnd_cols),
                          (brow_i[:, :], bnd_rows.broadcast_to([BP, NB])), (bmapv[:, :, 0], bnd_numbers)]
            mark = {}
            with nc.Block() as block:
                @block.vector
                def _(v):
                    n = [0]

                    def do(ins):
                        n[0] += 1
                        ins.then_inc(s_dv, 1)

                    def seen():
                        v.wait_ge(s_dv, n[0])

                    do(V.memset(ones3[:, :], 1.0))
                    do(V.memset(rec[:, :, :], 0.0))
                    do(V.memset(bmapv[:, :, :], 0.0))
                    mark["cleared"] = n[0]
                    v.wait_ge(s_el, 16 * len(edge_loads))
                    do(V.tensor_copy(edge_f[:, :, :], edge_i[:, :, :]))
                    do(V.tensor_copy(row_f[:, :, :], row_i[:, :, :]))
                    do(V.tensor_copy(bcol[:, :, :], bcol_i[:, :, :]))
                    do(V.tensor_copy(brow_f[:, :], brow_i[:, :]))
                    seen()
                    do(V.tensor_tensor(row_m[:, 0, :, :], row_f[:, :, :],
                                       row_f[:, :, 0:1].broadcast_to([GE, U, P]), ALU.is_equal))
                    do(V.tensor_tensor(row_m[:, 1, :, :], row_f[:, :, :],
                                       row_f[:, :, P - 1:P].broadcast_to([GE, U, P]), ALU.is_equal))
                    do(V.tensor_tensor(tmp[:, 0, :], f_dst, f_first, ALU.is_equal))
                    do(V.tensor_tensor(tmp[:, 1, :], f_dst, f_last, ALU.is_equal))
                    do(V.tensor_tensor(tmp[:, 2, :], f_dst, f_prev, ALU.is_equal))
                    do(V.tensor_tensor(tmp[:, 3, :], f_dst, f_nxt, ALU.not_equal))
                    do(V.tensor_scalar(tmp[:, 4, :], f_dst, -float(SKIP), None, ALU.add))
                    do(V.tensor_copy(rec[:, :, DST], f_dst))
                    do(V.tensor_copy(rec[:, :, NORM], wcol[:, :]))
                    do(V.tensor_copy(rec[:, :, MAPV], slots[:, :]))
                    seen()
                    do(V.tensor_scalar(f_first, f_dst, float(N - 1), None, ALU.min))
                    seen()
                    do(V.tensor_tensor(row_m[:, 2, :, :], row_m[:, 0, :, :], row_m[:, 1, :, :], ALU.mult))
                    do(V.tensor_tensor(tmp[:, 0, :], tmp[:, 0, :], tmp[:, 1, :], ALU.max))
                    do(V.tensor_tensor(tmp[:, 3, :], tmp[:, 3, :], tmp[:, 4, :], ALU.mult))
                    do(V.tensor_scalar(rec[:, :, CARRIED], tmp[:, 2, :], -FAR, None, ALU.mult))
                    do(V.tensor_copy(rec_i[:, :, DSTI], f_first))
                    seen()
                    do(V.tensor_tensor(row_m[:, 1, :, :], row_m[:, 1, :, :], row_m[:, 2, :, :], ALU.subtract))
                    do(V.tensor_scalar(tmp[:, 0, :], tmp[:, 0, :], -1.0, 1.0, ALU.mult, ALU.add))
                    seen()
                    mark["masks"] = n[0]
                    do(V.tensor_copy(rec[:, :, KEEP], tmp[:, 0, :]))
                    do(V.tensor_tensor(tmp[:, 3, :], tmp[:, 3, :], tmp[:, 0, :], ALU.mult))
                    seen()
                    do(V.tensor_scalar(tmp[:, 3, :], tmp[:, 3, :], float(SKIP), None, ALU.add))
                    seen()
                    do(V.tensor_copy(rec_i[:, :, OUTI], tmp[:, 3, :]))
                    do(V.tensor_scalar(tmp[:, 4, :], tmp[:, 3, :], float(W0 // 4), float(C // 4), ALU.mult, ALU.add))
                    seen()
                    do(V.tensor_copy(rec_i[:, :, MAPI], tmp[:, 4, :]))
                    mark["records"] = n[0]
                    do(V.tensor_tensor(btmp[:, 0, :], bcol[:, 0, :], bcol[:, 1, :], ALU.not_equal))
                    do(V.tensor_tensor(btmp[:, 1, :], bcol[:, 0, :], bcol[:, 2, :], ALU.not_equal))
                    do(V.tensor_scalar(btmp[:, 2, :], bcol[:, 0, :], -float(SKIP), None, ALU.add))
                    seen()
                    do(V.tensor_scalar(bcol[:, 2, :], bcol[:, 0, :], float(N - 1), None, ALU.min))
                    seen()
                    do(V.tensor_tensor(btmp[:, 2, :], btmp[:, 1, :], btmp[:, 2, :], ALU.mult))
                    do(V.tensor_copy(bclip[:, :], bcol[:, 2, :]))
                    seen()
                    do(V.tensor_scalar(btmp[:, 2, :], btmp[:, 2, :], float(SKIP), None, ALU.add))
                    seen()
                    do(V.tensor_copy(bout[:, :], btmp[:, 2, :]))
                    do(V.tensor_scalar(btmp[:, 1, :], btmp[:, 2, :], float(W0 // 4), float(C // 4), ALU.mult, ALU.add))
                    seen()
                    do(V.tensor_copy(bmapi[:, :], btmp[:, 1, :]))
                    for j in range(BJ):
                        do(V.tensor_scalar(far[:, j, :], brow_f[:, :], bcol[:, 0, j:j + 1], -FAR,
                                           ALU.not_equal, ALU.mult))
                        do(V.tensor_scalar(same[:, j, :], brow_f[:, :], bcol[:, 0, j:j + 1], btmp[:, 0, j:j + 1],
                                           ALU.is_equal, ALU.mult))
                    v.wait_ge(s_cl, 16 * len(consts))
                    do(V.tensor_copy(part[0][:, :, :], bias_rows[:, :, :]))
                    seen()
                    do(V.tensor_tensor(brest[:, :, :], bias_rows[:, :, :], part[0][:, :, :], ALU.subtract))
                    seen()
                    do(V.tensor_copy(part[1][:, :, :], brest[:, :, :]))
                    seen()
                    do(V.tensor_tensor(brest[:, :, :], brest[:, :, :], part[1][:, :, :], ALU.subtract))
                    seen()
                    do(V.tensor_copy(part[2][:, :, :], brest[:, :, :]))
                    seen()
                    do(V.tensor_scalar(brest[:, :, :], part[0][:, :, :], ident[0:3, 0:1], None, ALU.mult))
                    for k in (1, 2):
                        seen()
                        do(V.scalar_tensor_tensor(out=brest[:, :, :], in0=part[k][:, :, :], scalar=ident[0:3, k:k + 1],
                                                  in1=brest[:, :, :], op0=ALU.mult, op1=ALU.add))
                    seen()
                    for l in range(2 * LAYERS):
                        do(V.tensor_copy(brow3[l][:, :, :], brest[:, l:l + 1, :].broadcast_to([3, U, C])))
                    v.wait_ge(s_pe, 1)
                    do(V.tensor_copy(v_src[:, :, :], banks[0][:, 0:LAYERS, :]))
                    do(V.tensor_copy(v_dst[:, :, :], banks[1][:, 0:LAYERS, :]))
                    seen()
                    do(V.tensor_tensor(v_sum[:, :, :], v_src[:, :, :], v_dst[:, :, :], ALU.add))
                    seen()

                @block.tensor
                def _(pe):
                    pe.wait_ge(s_cl, 16 * len(consts))
                    for h in range(2):
                        for l in range(LAYERS):
                            k = h * LAYERS + l
                            last = T.matmul(banks[h][:, l, :], lhsT=att[:, k:k + 1].broadcast_to([C, P]),
                                            rhs=wT[:, l, :], start=True, stop=True)
                    last.then_inc(s_pe, 1)

                @block.sync
                def _(sp):
                    sp.wait_ge(s_dv, mark["cleared"])
                    with nc.allow_non_contiguous_dma("boundary numbers among padding"):
                        for to, of in edge_loads:
                            sp.dma_start(to, of).then_inc(s_el, 16)
                    for to, of in consts:
                        sp.dma_start(to, of).then_inc(s_cl, 16)
                    sp.wait_ge(s_dv, mark["masks"])
                    sp.dma_start(bmasks.rearrange("g r e -> g (r e)"),
                                 row_m[:, 0:2, :, :].rearrange("g r u e -> g (r u e)")).then_inc(s_st, 16)
                    sp.wait_ge(s_dv, mark["records"])
                    sp.dma_start(records.rearrange("g p w -> p g w"),
                                 rec[:, :, :].rearrange("p (g u) f -> p g (u f)", u=U)).then_inc(s_st, 16)
                    sp.wait_ge(s_st, 32)

        end_phase()

        def norm_sems(name):
            return {k: sem(f"{name}_{k}") for k in ("stats", "moments", "var", "root", "rstd", "shift", "done")}

        def norm_tiles(c, tag, n, u):
            return [dict(st=sb(f"{tag}_st{k}", [P, u, 6], f32, c), mv=sb(f"{tag}_mv{k}", [P, u, 2], f32, c),
                         sc=sb(f"{tag}_sc{k}", [P, 4, u], f32, c)) for k in range(n)]

        def norm_vector_a(v, z, t, rows, n, p, u):
            for k in range(u):
                last = V.bn_stats(t["st"][0:p, k, :], rows[0:p, k, :])
            last.then_inc(z["stats"], 1)
            v.wait_ge(z["stats"], n)
            settle(v)
            for k in range(u):
                last = V.bn_aggr(t["mv"][0:p, k, :], t["st"][0:p, k, :])
            last.then_inc(z["moments"], 1)
            v.wait_ge(z["moments"], n)
            V.tensor_scalar(t["sc"][0:p, 0, 0:u], t["mv"][0:p, 0:u, 1], EPS, None, ALU.add).then_inc(z["var"], 1)

        def norm_scalar_a(a, z, t, n, p, u):
            a.wait_ge(z["var"], n)
            S.activation(t["sc"][0:p, 1, 0:u], t["sc"][0:p, 0, 0:u], ACT.Sqrt).then_inc(z["root"], 1)

        def norm_vector_b(v, z, t, n, p, u):
            v.wait_ge(z["root"], n)
            V.reciprocal(t["sc"][0:p, 2, 0:u], t["sc"][0:p, 1, 0:u]).then_inc(z["rstd"], 1)
            v.wait_ge(z["rstd"], n)
            V.scalar_tensor_tensor(out=t["sc"][0:p, 3, 0:u], in0=t["mv"][0:p, 0:u, 0], scalar=-1.0,
                                   in1=t["sc"][0:p, 2, 0:u], op0=ALU.mult, op1=ALU.mult).then_inc(z["shift"], 1)

        def norm_scalar_b(a, z, t, rows, to, n, p, u):
            a.wait_ge(z["shift"], n)
            for k in range(u):
                last = S.activation(to[0:p, k, 0:C], rows[0:p, k, :], ACT.Relu,
                                    bias=t["sc"][0:p, 3, k:k + 1], scale=t["sc"][0:p, 2, k:k + 1])
            last.then_inc(z["done"], 1)

        def shape_of(g):
            return (TP, TU) if g.i is None and g.c - g.base == GN else (P, U)

        def node_rows(t, g, first=0):
            p, u = shape_of(g)
            return t[ds(g.at(P * U) + first, p * u), :].rearrange("(p u) c -> p u c", p=p)

        def slot_rows(t, g):
            return t[ds(g.at(P * U), P * U), :].rearrange("(p u) c -> p u c", p=P)

        def norm_pass(name, groups, load_from, store_to, width, un, peeled, numbers=None):
            z = norm_sems(name)
            z_ld, z_st = sems(f"{name}_loaded", un), sems(f"{name}_stored", un)
            if numbers:
                z_nx, z_nc = sem(f"{name}_next_numbers"), sem(f"{name}_numbered")
            with ExitStack() as c2:
                t = norm_tiles(c2, name, un, U)
                rows = [sb(f"{name}_rows{k}", [P, U, C], f32, c2) for k in range(un)]
                h = [sb(f"{name}_h{k}", [P, U, width], f32, c2) for k in range(un)]
                num = sb(f"{name}_num", [P, U], f32, c2)
                tnum = sb(f"{name}_tnum", [P, TU], f32, c2)
                with nc.Block() as block:
                    @block.sync
                    def _(sp):
                        if numbers:
                            sp.dma_start(num[:, :], node_numbers).then_inc(z_nc, 16)
                            sp.dma_start(tnum[0:TP, :], tail_numbers).then_inc(z_nc, 16)

                        def load(g):
                            p, u = shape_of(g) if numbers else (P, U)
                            after(sp, z["done"], g, un)
                            settle(sp)
                            sp.dma_start(rows[g.slot][0:p, 0:u, :], load_from(g)).then_inc(z_ld[g.slot], 16)

                        def store(g):
                            p, u = shape_of(g) if numbers else (P, U)
                            sp.wait_ge(z["done"], g.count())
                            settle(sp)
                            if numbers:
                                sp.wait_ge(z_nx, g.count(2))
                                settle(sp)
                            sp.dma_start(store_to(g), h[g.slot][0:p, 0:u, :]).then_inc(z_st[g.slot], 16)
                        pipeline(sp, groups, [(-1, load), (4, store)], un, last_peeled=peeled)
                        for k in range(un):
                            sp.wait_ge(z_st[k], 16 * ((groups - k + un - 1) // un))

                    @block.vector
                    def _(v):
                        if numbers:
                            for k in range(un):
                                V.memset(h[k][:, :, C:width], 0.0)
                            v.wait_ge(z_nc, 32)
                            V.tensor_scalar(num[:, :], num[:, :], 0.0, None, ALU.add).then_inc(z_nx, 1)

                        def first(g):
                            p, u = shape_of(g) if numbers else (P, U)
                            v.wait_ge(z_ld[g.slot], g.uses())
                            norm_vector_a(v, z, t[g.slot], rows[g.slot], g.count(), p, u)

                        def second(g):
                            p, u = shape_of(g) if numbers else (P, U)
                            norm_vector_b(v, z, t[g.slot], g.count(), p, u)
                            if numbers:
                                after_dma(v, z_st[g.slot], g)
                                v.wait_ge(z_nx, g.count())
                                if p == P:
                                    V.tensor_copy(h[g.slot][:, :, C], num[:, :]).then_inc(z_nc, 1)
                                    v.wait_ge(z_nc, g.count(33))
                                    V.tensor_scalar(num[:, :], num[:, :], float(P * U), None, ALU.add)\
                                     .then_inc(z_nx, 1)
                                else:
                                    V.tensor_copy(h[g.slot][0:p, 0:u, C], tnum[0:p, 0:u]).then_inc(z_nx, 1)
                        pipeline(v, groups, [(2, second), (0, first)], un, last_peeled=peeled)

                    @block.scalar
                    def _(a):
                        def first(g):
                            norm_scalar_a(a, z, t[g.slot], g.count(), *(shape_of(g) if numbers else (P, U)))

                        def second(g):
                            after_dma(a, z_st[g.slot], g)
                            norm_scalar_b(a, z, t[g.slot], rows[g.slot], h[g.slot], g.count(),
                                          *(shape_of(g) if numbers else (P, U)))
                        pipeline(a, groups, [(1, first), (3, second)], un, last_peeled=peeled)

        norm_pass("nodes_norm", GN + 1, lambda g: node_rows(x, g), lambda g: node_rows(tables[0], g),
                  W0, 8, 1, numbers=True)

        end_phase()

        d_ld, d_xl, d_st = sems("d_loaded", 4), sems("d_x_loaded", 4), [sems(f"d_stored{m}_", 2) for m in range(3)]
        d_t0, d_c0 = sem("d_transposed"), sem("d_copied")
        d_mm, d_sg, d_ad, d_tr, d_rw = (sems(f"d_{k}", 3) for k in ("product", "gate", "added", "back", "rows"))
        z = norm_sems("edges_norm")
        x_es, x_gx, x_rs, x_hs = (sems(f"x_{k}", UX) for k in ("records", "gathered", "rows_stored", "normed_stored"))
        with ExitStack() as c2:
            rows = [sb(f"d_rows{k}", [P, U, C], f32, c2) for k in range(4)]
            xr = [sb(f"d_xr{k}", [P, U, C], f32, c2) for k in range(4)]
            xT = [Ring([sb(f"d_xT{m}_{k}", [C, U, P], f32, c2) for k in range(4 if m < 3 else 2)]) for m in range(4)]
            sg = [[sb(f"d_sg{m}_{k}", [C, U, P], f32, c2) for k in range(2)] for m in range(3)]
            ro = [[sb(f"d_ro{m}_{k}", [P, U, C], f32, c2) for k in range(2)] for m in range(3)]
            t = norm_tiles(c2, "edges_norm", UX, U)
            es = [sb(f"x_es{k}", [P, U, NF], f32, c2) for k in range(UX)]
            edge_rows = [sb(f"x_rows{k}", [P, U, C], f32, c2) for k in range(UX)]
            h = [sb(f"x_h{k}", [P, U, C], f32, c2) for k in range(UX)]
            map_view = tables[0].rearrange("n (a w) -> (n a) w", w=4)

            def node_out(m, g):
                return node_rows(mid_nodes, g) if m == 2 else node_rows(tables[m + 1], g, NODE0)

            with nc.Block() as block:
                @block.sync
                def _(sp):
                    def load(g):
                        p, u = shape_of(g)
                        sp.wait_ge(d_t0, g.count())
                        settle(sp)
                        sp.dma_start(rows[g.slot % 4][0:p, 0:u, :], node_rows(tables[0], g)[:, :, 0:C])\
                          .then_inc(d_ld[g.slot % 4], 16)

                    def load_x(g):
                        p, u = shape_of(g)
                        sp.wait_ge(d_rw[2], g.count())
                        settle(sp)
                        sp.dma_start(xr[g.slot % 4][0:p, 0:u, :], node_rows(x, g)).then_inc(d_xl[g.slot % 4], 16)
                    sp.sem_inc(d_t0, 4)
                    sp.sem_inc(d_rw[2], 4)

                    def store(m):
                        def fn(g):
                            p, u = shape_of(g)
                            k = g.slot % 2
                            sp.wait_ge(d_rw[m], g.count(5 if m == 2 else 2))
                            settle(sp)
                            sp.dma_start(node_out(m, g), ro[m][k][0:p, 0:u, :]).then_inc(d_st[m][k], 16)
                        return fn
                    
                    def load_record(g):
                        after_dma(sp, x_gx[g.slot], g, 16 * U)
                        settle(sp)
                        sp.dma_start(es[g.slot][:, :, :], records[ds(g.at(1), 1), :, :].rearrange(
                            "a p w -> (a p) w")).then_inc(x_es[g.slot], 16)

                    def store_rows(g):
                        sp.wait_ge(x_gx[g.slot], g.uses(1, 16 * U))
                        settle(sp)
                        sp.dma_start(slot_rows(raw_rows, g), edge_rows[g.slot][:, :, :]).then_inc(x_rs[g.slot], 16)

                    def store_normed(g):
                        sp.wait_ge(z["done"], g.count())
                        settle(sp)
                        sp.dma_start(slot_rows(own0, g), h[g.slot][:, :, :]).then_inc(x_hs[g.slot], 16)
                    pipeline_pair(sp, [(0, load), (9, store(2)), (7, store(1)), (5, store(0)), (5, load_x)],
                                  [(0, load_record), (2, store_rows), (4, store_normed)])
                    for k in range(UX):
                        sp.wait_ge(x_rs[k], 16 * ((GE - k + UX - 1) // UX))
                        sp.wait_ge(x_hs[k], 16 * ((GE - k + UX - 1) // UX))
                    for m in range(3):
                        for k in range(2):
                            sp.wait_ge(d_st[m][k], 16 * ((GN + 2 - k) // 2))

                @block.gpsimd
                def _(q):
                    def gather(g):
                        b = g.slot
                        after_dma(q, x_rs[b], g)
                        settle(q)
                        after(q, z["done"], g, UX)
                        settle(q)
                        q.wait_ge(x_es[b], g.uses())
                        settle(q)
                        for u in range(U):
                            q.indirect_dma_start(
                                out=edge_rows[b][:, u, :], out_offset=None, in_=x,
                                in_offset=bass.IndirectOffsetOnAxis(
                                    ap=es[b][:, u, DSTI:DSTI + 1].bitcast(i32), axis=0),
                                bounds_check=N - 1, oob_is_err=False).then_inc(x_gx[b], 16)
                    pipeline(q, GE, [(0, gather)], UX)

                @block.tensor
                def _(pe):
                    def enter(g):
                        p, u = shape_of(g)
                        pe.wait_ge(d_ld[g.slot % 4], g.part_uses(4))
                        pe.wait_ge(d_c0, g.count())
                        for k in range(u):
                            last = T.transpose(banks[0][:, k, 0:p], rows[g.slot % 4][0:p, k, :], ident[0:p, 0:p])
                        last.then_inc(d_t0, 1)

                    def product(m):
                        def fn(g):
                            p, u = shape_of(g)
                            pe.wait_ge(d_c0 if m == 0 else d_ad[m - 1], g.count(2 if m == 0 else 1))
                            pe.wait_ge(d_sg[m], g.count())
                            T.matmul(banks[1 + m][:, 0:u, 0:p], lhsT=gat_w[:, m, :],
                                     rhs=xT[m][g][:, 0:u, 0:p], start=True, stop=True)\
                             .then_inc(d_mm[m], 1)
                        return fn

                    def back(m):
                        def fn(g):
                            p, u = shape_of(g)
                            pe.wait_ge(d_ad[m], g.count())
                            pe.wait_ge(d_rw[m], g.count(1 if m < 2 else 4))
                            for k in range(u):
                                last = T.transpose(banks[4 + m][0:p, k, :], xT[m + 1][g][:, k, 0:p],
                                                   ident[:, :])
                            last.then_inc(d_tr[m], 1)
                        return fn
                    pipeline(pe, GN + 1, [(7, back(2)), (5, product(2)), (5, back(1)), (3, product(1)), (3, back(0)),
                              (1, product(0)), (0, enter)], 8, last_peeled=1)

                @block.scalar
                def _(a):
                    a.sem_inc(d_c0, 1)
                    for m in range(3):
                        a.sem_inc(d_sg[m], 1)

                    def enter(g):
                        p, u = shape_of(g)
                        a.wait_ge(d_t0, g.count(5))
                        after(a, d_ad[0], g, 4)
                        S.activation(xT[0][g][:, 0:u, 0:p], banks[0][:, 0:u, 0:p], ACT.Copy)\
                         .then_inc(d_c0, 1)

                    def gate(m):
                        def fn(g):
                            p, u = shape_of(g)
                            a.wait_ge(d_mm[m], g.count())
                            after(a, d_ad[m], g, 2)
                            S.activation(sg[m][g.slot % 2][:, 0:u, 0:p], banks[1 + m][:, 0:u, 0:p], ACT.Sigmoid,
                                         bias=gat_b[:, m:m + 1]).then_inc(d_sg[m], 1)
                        return fn

                    def root(g):
                        norm_scalar_a(a, z, t[g.slot], g.count(), P, U)

                    def normed(g):
                        after_dma(a, x_hs[g.slot], g)
                        norm_scalar_b(a, z, t[g.slot], edge_rows[g.slot], h[g.slot], g.count(), P, U)
                    pipeline_pair(a, [(5, gate(2)), (3, gate(1)), (1, gate(0)), (0, enter)],
                                  [(3, normed), (2, root)])

                @block.vector
                def _(v):
                    v.sem_inc(d_rw[0], 1)
                    v.sem_inc(d_rw[1], 1)

                    def add(m):
                        def fn(g):
                            p, u = shape_of(g)
                            k = g.slot % 2
                            v.wait_ge(d_sg[m], g.count(2))
                            V.tensor_tensor(xT[m + 1][g][:, 0:u, 0:p], xT[m][g][:, 0:u, 0:p],
                                            sg[m][k][:, 0:u, 0:p], ALU.add).then_inc(d_ad[m], 1)
                        return fn

                    def rows_of(m):
                        def fn(g):
                            p, u = shape_of(g)
                            k, k4 = g.slot % 2, g.slot % 4
                            after_part(v, d_st[m][k], g, 2)
                            v.wait_ge(d_tr[m], g.count())
                            if m < 2:
                                V.tensor_copy(ro[m][k][0:p, 0:u, :], banks[4 + m][0:p, 0:u, :])\
                                 .then_inc(d_rw[m], 1)
                            else:
                                v.wait_ge(d_xl[k4], g.part_uses(4))
                                V.tensor_tensor(ro[m][k][0:p, 0:u, :], banks[4 + m][0:p, 0:u, :],
                                                xr[g.slot % 4][0:p, 0:u, :], ALU.add).then_inc(d_rw[m], 1)
                        return fn

                    def moments(g):
                        v.wait_ge(x_gx[g.slot], g.uses(1, 16 * U))
                        norm_vector_a(v, z, t[g.slot], edge_rows[g.slot], g.count(), P, U)

                    def scales(g):
                        norm_vector_b(v, z, t[g.slot], g.count(), P, U)
                    pipeline_pair(v, [(8, rows_of(2)), (6, add(2)), (6, rows_of(1)), (4, add(1)), (4, rows_of(0)), (2, add(0))],
                                  [(3, scales), (2, moments)])

        end_phase()

        zb = norm_sems("boundary_norm")
        b_gx, b_st = sem("boundary_gathered"), sem("boundary_stored")
        with ExitStack() as c2:
            tbn = norm_tiles(c2, "boundary_norm", 1, BJ)[0]
            hb = sb("boundary_h", [BP, BJ, C], f32, c2)

            def boundary_rows(table, first):
                return table[first:first + NB, :].rearrange("(j p) c -> p j c", p=BP)

            with nc.Block() as block:
                @block.gpsimd
                def _(q):
                    for j in range(BJ):
                        q.indirect_dma_start(
                            out=braw[:, j, :], out_offset=None, in_=x,
                            in_offset=bass.IndirectOffsetOnAxis(ap=bclip[:, j:j + 1], axis=0),
                            bounds_check=N - 1, oob_is_err=False).then_inc(b_gx, 16)
                    for j in range(BJ):
                        q.indirect_dma_start(
                            out=map_view, out_offset=bass.IndirectOffsetOnAxis(ap=bmapi[:, j:j + 1], axis=0),
                            in_=bmapv[:, j, :], in_offset=None,
                            bounds_check=N * (W0 // 4) - 1, oob_is_err=False).then_inc(b_st, 16)
                    q.wait_ge(zb["done"], 1)
                    settle(q)
                    q.dma_start(boundary_rows(own0, EP), hb[:, :, :]).then_inc(b_st, 16)
                    q.wait_ge(b_st, 16 * (BJ + 1))

                @block.vector
                def _(v):
                    v.wait_ge(b_gx, 16 * BJ)
                    norm_vector_a(v, zb, tbn, braw, 1, BP, BJ)
                    norm_vector_b(v, zb, tbn, 1, BP, BJ)

                @block.scalar
                def _(a):
                    norm_scalar_a(a, zb, tbn, 1, BP, BJ)
                    norm_scalar_b(a, zb, tbn, braw, hb, 1, BP, BJ)

        end_phase()

        m_es, m_mp = sems("map_records"), sems("mapped")
        zc = norm_sems("c_norm")
        c_ld, c_st = sems("c_loaded", 8), [sems(f"c_stored{m}_", 4) for m in range(4)]
        c_t0, c_c0 = sem("c_transposed"), sem("c_copied")
        c_mm, c_re, c_tr, c_rw = (sems(f"c_{k}", 3) for k in ("product", "relu", "back", "rows"))
        with ExitStack() as c2:
            t = norm_tiles(c2, "c_norm", 8, U)
            rows = [sb(f"c_rows{k}", [P, U, C], f32, c2) for k in range(8)]
            es = [sb(f"map_es{k}", [P, U, NF], f32, c2) for k in range(UX)]
            zr = [sb(f"c_zr{k}", [P, U, C], f32, c2) for k in range(4)]
            zT = [[sb(f"c_zT{m}_{k}", [C, U, P], f32, c2) for k in range(2)] for m in range(4)]
            ro = [[sb(f"c_ro{m}_{k}", [P, U, C], f32, c2) for k in range(4)] for m in range(3)]

            with nc.Block() as block:
                @block.sync
                def _(sp):
                    sp.sem_inc(c_rw[2], 8)

                    def load(g):
                        p, u = shape_of(g)
                        sp.wait_ge(c_rw[2], g.count())
                        settle(sp)
                        sp.dma_start(rows[g.slot][0:p, 0:u, :], node_rows(mid_nodes, g)).then_inc(c_ld[g.slot], 16)

                    def store_norm(g):
                        p, u = shape_of(g)
                        sp.wait_ge(zc["done"], g.count())
                        settle(sp)
                        sp.dma_start(node_rows(tables[3], g, NODE0), zr[g.slot % 4][0:p, 0:u, :])\
                         .then_inc(c_st[3][g.slot % 4], 16)

                    def store(m):
                        def fn(g):
                            p, u = shape_of(g)
                            k = g.slot % 4
                            sp.wait_ge(c_rw[m], g.count(1 + 8 * (m == 2) + (m < 2)))
                            to = node_rows(out, g) if m == 2 else node_rows(tables[4 + m], g, NODE0)
                            settle(sp)
                            sp.dma_start(to, ro[m][k][0:p, 0:u, :]).then_inc(c_st[m][k], 16)
                        return fn
                    pipeline(sp, GN + 1, [(-1, load), (7, store(2)), (6, store(1)), (5, store(0)), (2, store_norm)], 8,
                             last_peeled=1)
                    for m in range(4):
                        for k in range(4):
                            sp.wait_ge(c_st[m][k], 16 * ((GN + 4 - k) // 4))

                @block.gpsimd
                def _(q):
                    def load_record(g):
                        after_dma(q, m_mp[g.slot], g, 16 * U)
                        settle(q)
                        q.dma_start(es[g.slot][:, :, :], records[ds(g.at(1), 1), :, :].rearrange(
                            "a p w -> (a p) w")).then_inc(m_es[g.slot], 16)

                    def scatter(g):
                        q.wait_ge(m_es[g.slot], g.uses())
                        settle(q)
                        for u in range(U):
                            q.indirect_dma_start(
                                out=map_view, out_offset=bass.IndirectOffsetOnAxis(
                                    ap=es[g.slot][:, u, MAPI:MAPI + 1].bitcast(i32), axis=0),
                                in_=es[g.slot][:, u, MAPV:NF], in_offset=None,
                                bounds_check=N * (W0 // 4) - 1, oob_is_err=False).then_inc(m_mp[g.slot], 16)
                    pipeline(q, GE, [(2, scatter), (0, load_record)], UX)
                    for k in range(UX):
                        q.wait_ge(m_mp[k], 16 * U * ((GE - k + UX - 1) // UX))

                @block.vector
                def _(v):
                    def first(g):
                        v.wait_ge(c_ld[g.slot], g.uses())
                        norm_vector_a(v, zc, t[g.slot], rows[g.slot], g.count(), *shape_of(g))

                    def second(g):
                        norm_vector_b(v, zc, t[g.slot], g.count(), *shape_of(g))

                    def rows_of(m):
                        def fn(g):
                            p, u = shape_of(g)
                            k = g.slot % 4
                            after_part(v, c_st[m][k], g, 4)
                            v.wait_ge(c_tr[m], g.count())
                            if m < 2:
                                V.tensor_copy(ro[m][k][0:p, 0:u, :], banks[4 + m][0:p, 0:u, :])\
                                 .then_inc(c_rw[m], 1)
                            else:
                                V.tensor_tensor(ro[m][k][0:p, 0:u, :], banks[4 + m][0:p, 0:u, :],
                                                rows[g.slot][0:p, 0:u, :], ALU.add).then_inc(c_rw[m], 1)
                        return fn

                    def enter(g):
                        p, u = shape_of(g)
                        v.wait_ge(c_t0, g.count())
                        V.tensor_copy(zT[0][g.slot % 2][:, 0:u, 0:p], banks[0][:, 0:u, 0:p]).then_inc(c_c0, 1)
                    v.sem_inc(c_c0, 1)
                    v.sem_inc(c_rw[0], 1)
                    v.sem_inc(c_rw[1], 1)
                    pipeline(v, GN + 1, [(1, second), (3, enter), (0, first), (6, rows_of(2)), (5, rows_of(1)),
                                         (4, rows_of(0))], 8, last_peeled=1)

                @block.scalar
                def _(a):
                    for m in range(3):
                        a.sem_inc(c_re[m], 1)

                    def first(g):
                        norm_scalar_a(a, zc, t[g.slot], g.count(), *shape_of(g))

                    def second(g):
                        k = g.slot % 4
                        after_part(a, c_st[3][k], g, 4)
                        after(a, c_t0, g, 4)
                        norm_scalar_b(a, zc, t[g.slot], rows[g.slot], zr[k], g.count(), *shape_of(g))

                    def relu(m):
                        def fn(g):
                            p, u = shape_of(g)
                            a.wait_ge(c_mm[m], g.count())
                            S.activation(zT[m + 1][g.slot % 2][:, 0:u, 0:p], banks[1 + m][:, 0:u, 0:p], ACT.Relu,
                                         bias=node_b[:, m:m + 1]).then_inc(c_re[m], 1)
                        return fn
                    pipeline(a, GN + 1, [(1, second), (5, relu(2)), (4, relu(1)), (3, relu(0)), (0, first)], 8,
                             last_peeled=1)

                @block.tensor
                def _(pe):
                    def enter(g):
                        p, u = shape_of(g)
                        pe.wait_ge(zc["done"], g.count())
                        pe.wait_ge(c_c0, g.count())
                        for k in range(u):
                            last = T.transpose(banks[0][:, k, 0:p], zr[g.slot % 4][0:p, k, :], ident[0:p, 0:p])
                        last.then_inc(c_t0, 1)

                    def product(m):
                        def fn(g):
                            p, u = shape_of(g)
                            pe.wait_ge(c_c0 if m == 0 else c_re[m - 1], g.count(2))
                            pe.wait_ge(c_re[m], g.count())
                            T.matmul(banks[1 + m][:, 0:u, 0:p], lhsT=wn[m][:, 0, :],
                                     rhs=zT[m][g.slot % 2][:, 0:u, 0:p], start=True, stop=True)\
                             .then_inc(c_mm[m], 1)
                        return fn

                    def back(m):
                        def fn(g):
                            p, u = shape_of(g)
                            pe.wait_ge(c_re[m], g.count(2))
                            pe.wait_ge(c_rw[m], g.count(1 if m < 2 else 8))
                            for k in range(u):
                                last = T.transpose(banks[4 + m][0:p, k, :], zT[m + 1][g.slot % 2][:, k, 0:p],
                                                   ident[:, :])
                            last.then_inc(c_tr[m], 1)
                        return fn
                    pipeline(pe, GN + 1, [(6, back(2)), (5, product(2)), (5, back(1)), (4, product(1)), (4, back(0)),
                                          (3, product(0)), (2, enter)], 8, last_peeled=1)

        end_phase()

        def own_of(l):
            return own0 if l == 0 else tables[l]

        e_es, e_xd, e_gx, e_ex = (sems(f"e_{k}", UE) for k in ("records", "own", "gathered", "extra"))
        e_st, e_bs, e_lk = (sems(f"e_{k}_stored", UE) for k in ("rows", "bstats", "lookups"))

        def load_group(sp, g, l, t, extra=None):
            b = g.slot
            sp.dma_start(t["es"][g][:, :, :], records[ds(g.at(1), 1), :, :].rearrange("a p w -> (a p) w"))\
              .then_inc(e_es[b], 16)
            sp.dma_start(t["gi"][g][:, :], (src_lookups if l == 0 else lookups)[ds(g.at(1), 1), :, :].rearrange(
                "a p u -> (a p) u")).then_inc(e_es[b], 16)
            own = own_of(l)
            sp.dma_start(t["xd"][g][:, :, :], slot_rows(own, g)).then_inc(e_xd[b], 16)
            sp.dma_start(t["b2"][g][:, :, :], own[ds(g.at(2 * U) + EP, 2 * U), :].rearrange(
                "(r u) c -> r u c", r=2)).then_inc(e_xd[b], 16)
            sp.dma_start(t["fm"][g][:, :, :], bmasks[ds(g.at(1), 1), :, :].rearrange(
                "a r (u e) -> (a r) u e", u=U)).then_inc(e_xd[b], 16)

        def gather_group(q, g, l, t):
            b = g.slot
            q.wait_ge(e_es[b], g.uses(1, 32))
            settle(q)
            width = W0 if l == 0 else C
            for u in range(U):
                q.indirect_dma_start(out=t["xs"][g][:, u, 0:width], out_offset=None, in_=tables[l],
                                     in_offset=bass.IndirectOffsetOnAxis(ap=t["gi"][g][:, u:u + 1], axis=0),
                                     bounds_check=(N if l == 0 else ROWS) - 1, oob_is_err=False)\
                 .then_inc(e_gx[b], 16)

        def tiles_of(c, tag, names, **fewer):
            shapes = dict(es=([P, U, NF], f32), gi=([P, U], i32), xs=([P, U, W0], f32), b2=([2, U, C], f32),
                          fm=([2, U, P], f32), zz=([P, 2, U], f32), dd=([P, U], f32), ev=([P, 2, U], f32),
                          ml=([P, 2, U], f32), arg=([P, 2, U], f32), w=([P, 2, U], f32), rl=([P, U], f32),
                          al=([P, 2, U], f32), li=([P, U], i32),
                          oi=([P, U], i32))
            return {n: Ring([sb(f"{tag}_{n}{k}", *shapes.get(n, ([P, U, P], f32)), c) for k in range(fewer.get(n, UE))])
                    for n in names}

        def bc(ap):
            return ap.unsqueeze(2).broadcast_to([P, U, P])

        def tile_matrix_rows(pe, g, t):
            for u in range(U):
                last = T.transpose(banks[0][:, u, :], t["es"][g][:, u, DST:DST + 1].broadcast_to([P, P]),
                                   ident[:, :])
            return last

        def boundary_values(pe, g, t):
            for u in range(U):
                last = T.matmul(banks[1][:, u, :], lhsT=t["fm"][g][0:2, u, :], rhs=t["b2"][g][0:2, u, :],
                                start=True, stop=True)
            return last

        def put_boundary_values(v, g, t):
            for u in range(U):
                last = V.scalar_tensor_tensor(out=t["xd"][g][:, u, :], in0=t["xd"][g][:, u, :],
                                              scalar=t["es"][g][:, u, KEEP:KEEP + 1], in1=banks[1][:, u, :],
                                              op0=ALU.mult, op1=ALU.add)
            return last

        def export(v, g, aT):
            return V.tensor_copy(bexp[:, ds(g.at(2 * U), 2 * U)].rearrange("c (r u) -> c r u", r=2),
                                 aT[:, :, 0:P:P - 1].rearrange("c u r -> c r u"))

        a_ = {k: sem(f"gat_{k}") for k in (
            "dst_rows", "boundary", "own", "same", "far", "dots", "logit", "leaky", "logits", "logit_rows", "max",
            "arg", "weights", "sums", "total", "inverse", "alpha", "matrix", "diagonal", "aggregate", "columns",
            "product", "tanh", "half", "gate", "rows", "exported", "lookup", "sum")}

        def gat_pass(l):
            base = GE * l
            kinds = ["es", "gi", "xs", "b2", "fm", "zz", "dd", "ev", "ml", "arg", "w", "rl", "al", "xd", "S", "far",
                     "D", "aT", "xh", "hf", "th", "xn"]
            kinds += ["li"] if l == 0 else []
            kinds += ["xr", "xo"] if l == LAYERS - 1 else []
            with ExitStack() as c2:
                t = tiles_of(c2, f"g{l}", kinds, far=2, D=2, aT=2, xh=3, hf=3, th=2, xn=3, xo=3)
                junk = sb(f"g{l}_junk", [P, 4 * U, P], f32, c2)
                final = "xo" if l == LAYERS - 1 else "xn"
                done = a_["sum"] if l == LAYERS - 1 else a_["rows"]

                def count_done(g, more=1):
                    return g.count(more - (base if l == LAYERS - 1 else 0))

                with nc.Block() as block:
                    @block.sync
                    def _(sp):
                        def load(g):
                            after(sp, a_["aggregate"], g, UE)
                            settle(sp)
                            after(sp, a_["half"], g, UE)
                            settle(sp)
                            load_group(sp, g, l, t)

                        def load_x(g):
                            if g.i is not None or g.c - base >= UE:
                                sp.wait_ge(a_["sum"], g.count(1 - UE - base))
                                settle(sp)
                            sp.dma_start(t["xr"][g][:, :, :], slot_rows(raw_rows, g)).then_inc(e_ex[g.slot], 16)

                        def store(g):
                            b = g.slot
                            sp.wait_ge(a_["total"], g.count())
                            settle(sp)
                            sp.dma_start(bstats[:, ds(g.at(2 * U), 2 * U)].rearrange("k (r u) -> r k u", r=2),
                                         t["ml"][g][0:P:P - 1, :, :]).then_inc(e_bs[b], 16)
                            if l == 0:
                                sp.wait_ge(a_["lookup"], g.count())
                                settle(sp)
                                sp.dma_start(lookups[ds(g.at(1), 1), :, :].rearrange("a p u -> (a p) u"),
                                             t["li"][g][:, :]).then_inc(e_lk[b], 16)
                            sp.wait_ge(done, count_done(g))
                            to = mid_rows if l == LAYERS - 1 else tables[l + 1]
                            settle(sp)
                            sp.dma_start(slot_rows(to, g), t[final][g][:, :, :]).then_inc(e_st[b], 16)
                        pipeline(sp, GE, [(0, load), (8, store)] + ([(3, load_x)] if l == LAYERS - 1 else []), UE, base)
                        for k in range(UE):
                            end = Turn(None, base + GE - UE + (k - (base + GE - UE)) % UE, UE, base)
                            sp.wait_ge(e_bs[k], end.uses())
                            sp.wait_ge(e_st[k], end.uses())
                            if l == 0:
                                sp.wait_ge(e_lk[k], end.uses())

                    @block.gpsimd
                    def _(q):
                        def update(g):
                            if l < LAYERS - 1:
                                after_dma_of(q, e_st, g, 3)
                            elif g.i is not None or g.c - base >= 3:
                                q.wait_ge(a_["sum"], g.count(-2 - base))
                            settle(q)
                            q.wait_ge(a_["half"], g.count())
                            settle(q)
                            q.wait_ge(a_["gate"], g.count())
                            settle(q)
                            Q.tensor_tensor(t["xn"][g][:, :, :], t["hf"][g][:, :, :], t["xh"][g][:, :, :], ALU.add)\
                             .then_inc(a_["rows"], 1)
                        pipeline(q, GE, [(0, lambda g: gather_group(q, g, l, t)), (6, update)], UE, base)

                    @block.tensor
                    def _(pe):
                        def aggregate(g):
                            b = g.slot
                            pe.wait_ge(a_["matrix"], g.count())
                            pe.wait_ge(a_["diagonal"], g.count())
                            after(pe, a_["columns"], g)
                            for u in range(U):
                                T.matmul(banks[4][:, u, :], lhsT=t["xs"][g][:, u, 0:C], rhs=t["S"][g][:, u, :],
                                         start=True, stop=False)
                                last = T.matmul(banks[4][:, u, :], lhsT=t["xd"][g][:, u, :], rhs=t["D"][g][:, u, :],
                                                start=False, stop=True)
                            last.then_inc(a_["aggregate"], 1)

                        def logit_rows(g):
                            pe.wait_ge(a_["logits"], g.count())
                            after(pe, a_["max"], g)
                            for u in range(U):
                                last = T.transpose(banks[2][:, u, :], t["ev"][g][:, 0, u:u + 1].broadcast_to([P, P]),
                                                   ident[:, :])
                            last.then_inc(a_["logit_rows"], 1)

                        def enter(g):
                            pe.wait_ge(e_es[g.slot], g.uses(1, 32))
                            after(pe, a_["same"], g)
                            tile_matrix_rows(pe, g, t).then_inc(a_["dst_rows"], 1)
                            pe.wait_ge(e_xd[g.slot], g.uses(1, 48))
                            after(pe, a_["own"], g)
                            boundary_values(pe, g, t).then_inc(a_["boundary"], 1)

                        def sums(g):
                            b = g.slot
                            pe.wait_ge(a_["weights"], g.count())
                            after(pe, a_["total"], g)
                            for u in range(U):
                                last = T.matmul(banks[3][:, 0, u:u + 1], lhsT=t["S"][g][:, u, :],
                                                rhs=t["w"][g][:, 0, u:u + 1], start=True, stop=True)
                            last.then_inc(a_["sums"], 1)

                        def product(g):
                            b = g.slot
                            pe.wait_ge(a_["columns"], g.count())
                            after(pe, a_["tanh"], g)
                            T.matmul(banks[5][:, :, :], lhsT=ones3[:, :], rhs=brow3[l][:, :, :], start=True, stop=False,
                                     skip_group_check=True)
                            for u in range(U):
                                last = T.matmul(banks[5][:, u, :], lhsT=t["aT"][g][:, u, :], rhs=gat_w[:, l, :],
                                                start=False, stop=True, skip_group_check=True)
                            last.then_inc(a_["product"], 1)
                        pipeline(pe, GE, [(4, logit_rows), (2, enter), (6, product), (4, sums), (5, aggregate)], UE, base)

                    @block.scalar
                    def _(a):
                        def columns(g):
                            a.wait_ge(a_["aggregate"], g.count())
                            after(a, a_["exported"], g, 2)
                            S.activation(t["aT"][g][:, :, :], banks[4][:, :, :], ACT.Copy).then_inc(a_["columns"], 1)

                        def weights(g):
                            a.wait_ge(a_["arg"], g.count())
                            S.activation(t["w"][g][:, :, :], t["arg"][g][:, :, :], ACT.Exp)\
                             .then_inc(a_["weights"], 1)

                        def half(g):
                            a.wait_ge(a_["own"], g.count())
                            after(a, a_["rows"], g, 3)
                            S.activation(t["xh"][g][:, :, :], t["xd"][g][:, :, :], ACT.Copy, bias=0.5)\
                             .then_inc(a_["half"], 1)

                        def gate(g):
                            a.wait_ge(a_["tanh"], g.count())
                            after(a, a_["rows"], g, 3)
                            S.activation(t["hf"][g][:, :, :], t["th"][g][:, :, :], ACT.Copy, scale=0.5)\
                             .then_inc(a_["gate"], 1)

                        def tanh(g):
                            a.wait_ge(a_["product"], g.count())
                            after(a, a_["gate"], g, 2)
                            S.activation(t["th"][g][:, :, :], banks[5][:, :, :], ACT.Tanh, scale=0.5)\
                             .then_inc(a_["tanh"], 1)

                        def far_of(g):
                            a.wait_ge(a_["same"], g.count())
                            after(a, a_["max"], g, 2)
                            S.activation(t["far"][g][:, :, :], t["S"][g][:, :, :], ACT.Copy, bias=-FAR, scale=FAR)\
                             .then_inc(a_["far"], 1)

                        def matrices(g):
                            a.wait_ge(a_["alpha"], g.count())
                            for u in range(U):
                                last = S.activation(t["S"][g][:, u, :], t["S"][g][:, u, :], ACT.Copy,
                                                    scale=t["al"][g][:, 0, u:u + 1])
                            last.then_inc(a_["matrix"], 1)
                            for u in range(U):
                                last = S.activation(t["D"][g][:, u, :], ident[:, :], ACT.Copy,
                                                    scale=t["al"][g][:, 1, u:u + 1])
                            last.then_inc(a_["diagonal"], 1)
                        pipeline(a, GE, [(5, matrices), (4, weights), (6, tanh), (3, far_of), (6, gate), (5, half), (5, columns)], UE, base)

                    @block.vector
                    def _(v):
                        def maxima(g):
                            b = g.slot
                            v.wait_ge(a_["far"], g.count())
                            after_dma(v, e_bs[b], g)
                            v.wait_ge(a_["logit_rows"], g.count())
                            settle(v)
                            for u in range(U):
                                last = V.tensor_tensor_reduce(
                                    out=junk[:, 3 * U + u, :], in0=banks[2][:, u, :], in1=t["far"][g][:, u, :], scale=1.0,
                                    scalar=t["ev"][g][:, 1, u:u + 1], op0=ALU.add, op1=ALU.max,
                                    accum_out=t["ml"][g][:, 0, u:u + 1])
                            last.then_inc(a_["max"], 1)

                        def own_rows(g):
                            v.wait_ge(e_es[g.slot], g.uses(1, 32))
                            v.wait_ge(a_["boundary"], g.count())
                            put_boundary_values(v, g, t).then_inc(a_["own"], 1)

                        def argument(g):
                            v.wait_ge(a_["max"], g.count())
                            V.tensor_tensor(t["arg"][g][:, :, :], t["ev"][g][:, :, :],
                                            t["ml"][g][:, 0:1, :].broadcast_to([P, 2, U]), ALU.subtract)\
                             .then_inc(a_["arg"], 1)

                        def matrix(g):
                            v.wait_ge(a_["dst_rows"], g.count())
                            V.tensor_tensor(t["S"][g][:, :, :], banks[0][:, :, :], bc(t["es"][g][:, :, DST]),
                                            ALU.is_equal).then_inc(a_["same"], 1)

                        def dots(g):
                            b = g.slot
                            v.wait_ge(e_gx[b], g.uses(1, 16 * U))
                            if l == 0:
                                after_dma(v, e_lk[b], g)
                                V.tensor_copy(t["li"][g][:, :], t["xs"][g][:, :, C]).then_inc(a_["lookup"], 1)
                            v.wait_ge(a_["own"], g.count())
                            for u in range(U):
                                for k, (row, vec, to) in enumerate((
                                        (t["xs"], v_src, t["zz"][g][:, 0, u:u + 1]),
                                        (t["xd"], v_sum, t["zz"][g][:, 1, u:u + 1]),
                                        (t["xd"], v_dst, t["dd"][g][:, u:u + 1]))):
                                    last = V.tensor_tensor_reduce(
                                        out=junk[:, k * U + u, :], in0=row[g][:, u, 0:C], in1=vec[:, l, :], scale=1.0,
                                        scalar=0.0, op0=ALU.mult, op1=ALU.add, accum_out=to)
                            last.then_inc(a_["dots"], 1)

                        def total(g):
                            v.wait_ge(a_["sums"], g.count())
                            V.tensor_tensor(t["ml"][g][:, 1, :], banks[3][:, 0, 0:U], t["w"][g][:, 1, :], ALU.add)\
                             .then_inc(a_["total"], 1)

                        def logit(g):
                            v.wait_ge(a_["dots"], g.count())
                            V.tensor_tensor(t["zz"][g][:, 0, :], t["zz"][g][:, 0, :], t["dd"][g][:, :], ALU.add)\
                             .then_inc(a_["logit"], 1)

                        def inverse(g):
                            v.wait_ge(a_["total"], g.count())
                            V.reciprocal(t["rl"][g][:, :], t["ml"][g][:, 1, :]).then_inc(a_["inverse"], 1)

                        def leaky(g):
                            v.wait_ge(a_["logit"], g.count())
                            V.scalar_tensor_tensor(out=t["ev"][g][:, :, :], in0=t["zz"][g][:, :, :], scalar=SLOPE,
                                                   in1=t["zz"][g][:, :, :], op0=ALU.mult, op1=ALU.max)\
                             .then_inc(a_["leaky"], 1)

                        def alpha(g):
                            v.wait_ge(a_["inverse"], g.count())
                            V.tensor_tensor(t["al"][g][:, :, :], t["w"][g][:, :, :],
                                            t["rl"][g][:, :].unsqueeze(1).broadcast_to([P, 2, U]), ALU.mult)\
                             .then_inc(a_["alpha"], 1)

                        def carried(g):
                            v.wait_ge(a_["leaky"], g.count())
                            V.tensor_tensor(t["ev"][g][:, 1, :], t["ev"][g][:, 1, :], t["es"][g][:, :, CARRIED],
                                            ALU.add).then_inc(a_["logits"], 1)

                        def leave(g):
                            b = g.slot
                            v.wait_ge(a_["columns"], g.count())
                            export(v, g, t["aT"][g]).then_inc(a_["exported"], 1)

                        def add_x(g):
                            b = g.slot
                            v.wait_ge(e_ex[b], g.uses(since=base))
                            v.wait_ge(a_["rows"], g.count())
                            after_dma_of(v, e_st, g, 3)
                            V.tensor_tensor(t["xo"][g][:, :, :], t["xn"][g][:, :, :], t["xr"][g][:, :, :], ALU.add)\
                             .then_inc(a_["sum"], 1)
                        pipeline(v, GE, [
                            (4, maxima), (4, argument), (3, dots), (4, total), (3, logit), (4, inverse), (3, leaky),
                            (4, alpha), (3, carried), (2, own_rows), (2, matrix), (6, leave)]
                            + ([(7, add_x)] if l == LAYERS - 1 else []), UE, base)

        n_ = {k: sem(f"net_{k}") for k in (
            "dst_rows", "boundary", "own", "matrix", "src_t", "src_c", "own_t", "own_c", "edge", "edge_relu",
            "edge_t", "edge_c", "aggregate", "columns", "node", "rows", "exported", "sum")}
        n_ea, n_es, n_sc = (sems(f"n_{k}", UE) for k in (
            "edge_feats_loaded", "edge_feats_stored", "scattered"))

        def net_pass(l):
            L = LAYERS + l
            base = GE * L
            nbase = GE * LAYERS
            last_layer = l == LAYERS - 1
            kinds = ["es", "gi", "xs", "xd", "b2", "fm", "A", "sT", "dT", "eT", "eR", "aT", "xn"]
            kinds += ["ea"] if l else []
            kinds += ["xm", "xo", "oi"] if last_layer else []

            def cnt(g, more=1):
                return g.count(more - nbase)

            def aft(eng, s, g, back=1):
                if g.i is not None or g.c - nbase >= back:
                    eng.wait_ge(s, cnt(g, 1 - back))

            with ExitStack() as c2:
                t = tiles_of(c2, f"n{l}", kinds, A=3, sT=2, dT=3, eT=3, eR=2, aT=2, xn=3, xo=3, oi=3)
                with nc.Block() as block:
                    @block.sync
                    def _(sp):
                        def load(g):
                            b = g.slot
                            aft(sp, n_["edge"], g, UE)
                            settle(sp)
                            if last_layer and (g.i is not None or g.c - base >= UE):
                                sp.wait_ge(n_["sum"], cnt(g, 1 - UE - GE * l))
                                settle(sp)
                            load_group(sp, g, L, t)
                            if l:
                                sp.dma_start(t["ea"][g][:, :, :], edge_feats[ds(g.at(1), 1), :, :].rearrange(
                                    "a c (u e) -> (a c) u e", u=U)).then_inc(n_ea[b], 16)
                            if last_layer:
                                sp.dma_start(t["xm"][g][:, :, :], slot_rows(mid_rows, g)).then_inc(e_ex[b], 16)

                        def store(g):
                            b = g.slot
                            if not last_layer:
                                sp.wait_ge(n_["edge_relu"], cnt(g))
                                settle(sp)
                                sp.dma_start(edge_feats[ds(g.at(1), 1), :, :].rearrange("a c (u e) -> (a c) u e", u=U),
                                             t["eT"][g][:, :, :]).then_inc(n_es[b], 16)
                                sp.wait_ge(n_["rows"], cnt(g))
                                settle(sp)
                                sp.dma_start(slot_rows(tables[L + 1], g), t["xn"][g][:, :, :]).then_inc(e_st[b], 16)
                        pipeline(sp, GE, [(0, load), (5, store)], UE, base)
                        if not last_layer:
                            for k in range(UE):
                                end = Turn(None, base + GE - UE + (k - (base + GE - UE)) % UE, UE, base)
                                sp.wait_ge(e_st[k], end.uses())
                                sp.wait_ge(n_es[k], end.uses(since=nbase))

                    @block.gpsimd
                    def _(q):
                        def scatter(g):
                            b = g.slot
                            q.wait_ge(n_["sum"], cnt(g, 1 - GE * l))
                            settle(q)
                            for u in range(U):
                                q.indirect_dma_start(
                                    out=out, out_offset=bass.IndirectOffsetOnAxis(
                                        ap=t["oi"][g][:, u:u + 1], axis=0),
                                    in_=t["xo"][g][:, u, :], in_offset=None,
                                    bounds_check=N - 1, oob_is_err=False).then_inc(n_sc[b], 16)
                        work = [(0, lambda g: gather_group(q, g, L, t))]
                        pipeline(q, GE, work + ([(5, scatter)] if last_layer else []), UE, base)
                        if last_layer:
                            for k in range(UE):
                                end = Turn(None, base + GE - UE + (k - (base + GE - UE)) % UE, UE, base)
                                q.wait_ge(n_sc[k], end.uses(1, 16 * U, since=base))

                    @block.tensor
                    def _(pe):
                        def aggregate(g):
                            b = g.slot
                            pe.wait_ge(n_["edge_c"], cnt(g))
                            pe.wait_ge(n_["matrix"], cnt(g))
                            aft(pe, n_["columns"], g)
                            for u in range(U):
                                last = T.matmul(banks[6][:, u, :], lhsT=t["eR"][g][:, u, :], rhs=t["A"][g][:, u, :],
                                                start=True, stop=True)
                            last.then_inc(n_["aggregate"], 1)

                        def edge(g):
                            b = g.slot
                            pe.wait_ge(n_["src_c"], cnt(g))
                            pe.wait_ge(n_["own_c"], cnt(g))
                            if l:
                                pe.wait_ge(n_ea[b], g.uses(since=base - GE * (l - 1)))
                            aft(pe, n_["edge_relu"], g)
                            parts = [t["sT"], t["dT"]] + ([t["ea"]] if l else [])
                            for k, part in enumerate(parts):
                                last = T.matmul(banks[4][:, :, :], lhsT=we[l][:, k, :], rhs=part[g][:, :, :],
                                                start=k == 0, stop=k == len(parts) - 1)
                            last.then_inc(n_["edge"], 1)

                        def enter(g):
                            b = g.slot
                            pe.wait_ge(e_es[b], g.uses(1, 32))
                            aft(pe, n_["matrix"], g)
                            tile_matrix_rows(pe, g, t).then_inc(n_["dst_rows"], 1)
                            pe.wait_ge(e_xd[b], g.uses(1, 48))
                            aft(pe, n_["own"], g)
                            boundary_values(pe, g, t).then_inc(n_["boundary"], 1)
                            pe.wait_ge(e_gx[b], g.uses(1, 16 * U))
                            aft(pe, n_["src_c"], g)
                            for u in range(U):
                                last = T.transpose(banks[2][:, u, :], t["xs"][g][:, u, 0:C], ident[:, :])
                            last.then_inc(n_["src_t"], 1)

                        def edge_rows(g):
                            pe.wait_ge(n_["edge_relu"], cnt(g))
                            aft(pe, n_["edge_c"], g)
                            for u in range(U):
                                last = T.transpose(banks[5][:, u, :], t["eT"][g][:, u, :], ident[:, :])
                            last.then_inc(n_["edge_t"], 1)

                        def node(g):
                            b = g.slot
                            pe.wait_ge(n_["columns"], cnt(g))
                            aft(pe, n_["rows"], g)
                            T.matmul(banks[7][:, :, :], lhsT=ones3[:, :], rhs=brow3[L][:, :, :], start=True, stop=False,
                                     skip_group_check=True)
                            for u in range(U):
                                T.matmul(banks[7][:, u, :], lhsT=t["dT"][g][:, u, :], rhs=wn[l][:, 0, :],
                                         start=False, stop=False, skip_group_check=True)
                                last = T.matmul(banks[7][:, u, :], lhsT=t["aT"][g][:, u, :], rhs=wn[l][:, 1, :],
                                                start=False, stop=True, skip_group_check=True)
                            last.then_inc(n_["node"], 1)

                        def own_columns(g):
                            pe.wait_ge(n_["own"], cnt(g))
                            aft(pe, n_["own_c"], g)
                            for u in range(U):
                                last = T.transpose(banks[3][:, u, :], t["xd"][g][:, u, :], ident[:, :])
                            last.then_inc(n_["own_t"], 1)
                        pipeline(pe, GE, [(4, aggregate), (3, edge), (2, enter), (3, edge_rows), (4, node),
                                          (2, own_columns)], UE, base)

                    @block.scalar
                    def _(a):
                        def columns(g):
                            a.wait_ge(n_["aggregate"], cnt(g))
                            aft(a, n_["exported"], g, 2)
                            S.activation(t["aT"][g][:, :, :], banks[6][:, :, :], ACT.Copy).then_inc(n_["columns"], 1)

                        def edge_relu(g):
                            if not last_layer:
                                after_dma_of(a, n_es, g, 3, 16, nbase)
                            a.wait_ge(n_["edge"], cnt(g))
                            S.activation(t["eT"][g][:, :, :], banks[4][:, :, :], ACT.Relu,
                                         bias=edge_b[:, l:l + 1]).then_inc(n_["edge_relu"], 1)

                        def src_columns(g):
                            a.wait_ge(n_["src_t"], cnt(g))
                            S.activation(t["sT"][g][:, :, :], banks[2][:, :, :], ACT.Copy).then_inc(n_["src_c"], 1)

                        def rows(g):
                            if last_layer:
                                aft_last(a, g)
                            else:
                                after_dma_of(a, e_st, g, 3)
                            a.wait_ge(n_["node"], cnt(g))
                            S.activation(t["xn"][g][:, :, :], banks[7][:, :, :], ACT.Relu).then_inc(n_["rows"], 1)

                        def aft_last(a, g):
                            if g.i is not None or g.c - base >= 3:
                                a.wait_ge(n_["sum"], cnt(g, 1 - 3 - GE * l))
                        pipeline(a, GE, [(4, columns), (3, edge_relu), (2, src_columns), (4, rows)], UE, base)

                    @block.vector
                    def _(v):
                        def enter(g):
                            b = g.slot
                            v.wait_ge(e_es[b], g.uses(1, 32))
                            v.wait_ge(n_["dst_rows"], cnt(g))
                            for u in range(U):
                                last = V.tensor_scalar(t["A"][g][:, u, :], banks[0][:, u, :],
                                                       t["es"][g][:, u, DST:DST + 1], t["es"][g][:, u, NORM:NORM + 1],
                                                       ALU.is_equal, ALU.mult)
                            last.then_inc(n_["matrix"], 1)
                            v.wait_ge(n_["boundary"], cnt(g))
                            put_boundary_values(v, g, t).then_inc(n_["own"], 1)

                        def edge_copy(g):
                            v.wait_ge(n_["edge_t"], cnt(g))
                            V.tensor_copy(t["eR"][g][:, :, :], banks[5][:, :, :]).then_inc(n_["edge_c"], 1)

                        def leave(g):
                            b = g.slot
                            v.wait_ge(n_["columns"], cnt(g))
                            export(v, g, t["aT"][g]).then_inc(n_["exported"], 1)

                        def own_copy(g):
                            v.wait_ge(n_["own_t"], cnt(g))
                            V.tensor_copy(t["dT"][g][:, :, :], banks[3][:, :, :]).then_inc(n_["own_c"], 1)

                        def add(g):
                            b = g.slot
                            after_dma_of(v, n_sc, g, 3, 16 * U, base)
                            v.wait_ge(e_ex[b], g.uses(since=base, before=uses_before(GE * (LAYERS - 1), b)))
                            V.tensor_copy(t["oi"][g][:, :], t["es"][g][:, :, OUTI].bitcast(i32))
                            v.wait_ge(n_["rows"], cnt(g))
                            V.tensor_tensor(t["xo"][g][:, :, :], t["xn"][g][:, :, :], t["xm"][g][:, :, :], ALU.add)\
                             .then_inc(n_["sum"], 1)
                        pipeline(v, GE, [(2, enter), (3, edge_copy), (4, leave), (2, own_copy)]
                                 + ([(4, add)] if last_layer else []), UE, base)

        b_ = {k: sem(f"bnd_{k}") for k in ("loaded", "rows", "scaled", "max", "exp", "scale", "total", "inv",
                                            "sum", "sum_t", "sum_c", "out", "act", "half", "new", "stored", "scattered", "own_t",
                                            "own_c", "mid")}
        b_count = dict.fromkeys(b_, 0)

        def boundary_pass(L):
            gat = L < LAYERS
            l = L % LAYERS
            ends = L == 2 * LAYERS - 1
            W = C + 1 if gat else C

            def halves(k0, j):
                return banks[k0 + j // 4], j % 4

            at = dict(b_count)

            def up(k, n=1):
                b_count[k] += n
                return b_count[k]

            with ExitStack() as c2:
                xb = sb(f"b{L}_x", [BP, BJ, C], f32, c2)
                ex = sb(f"b{L}_ex", [BP, BJ, W], f32, c2)
                tot = sb(f"b{L}_tot", [BP, BJ, C], f32, c2)
                totT = sb(f"b{L}_totT", [C, BJ, BP], f32, c2)
                ownT = sb(f"b{L}_ownT", [C, BJ, BP], f32, c2)
                act = sb(f"b{L}_act", [BP, BJ, C], f32, c2)
                new = sb(f"b{L}_new", [BP, BJ, C], f32, c2)
                nrm = sb(f"b{L}_nrm", [BP, BJ, C], f32, c2)
                junk = sb(f"b{L}_junk", [BP, BJ if gat else 1, NB], f32, c2)
                mrow = sb(f"b{L}_mrow", [BP, NB], f32, c2)
                sc = sb(f"b{L}_sc", [BP, 6, BJ], f32, c2)
                tn = norm_tiles(c2, f"b{L}", 1, BJ)[0]
                zn = norm_sems(f"b{L}_norm") if L == LAYERS - 1 else None
                loads = [(xb[:, :, :], boundary_rows(own_of(L), EP))]
                if gat:
                    loads += [(sc[:, 0:2, :], bstats.rearrange("k (j p) -> p k j", p=BP)),
                              (mrow[:, :], bstats[0:1, :].broadcast_to([BP, NB]))]
                n_load = up("loaded", 16 * len(loads))
                v_rows, v_scaled = up("rows"), up("scaled")
                with nc.Block() as block:
                    @block.sync
                    def _(sp):
                        with nc.allow_non_contiguous_dma("statistics by partition"):
                            for to, of in loads:
                                sp.dma_start(to, of).then_inc(b_["loaded"], 16)
                        if not ends:
                            if L == LAYERS - 1:
                                sp.wait_ge(zn["done"], 1)
                                settle(sp)
                                sp.dma_start(boundary_rows(tables[L + 1], EP), nrm[:, :, :]).then_inc(b_["stored"], 16)
                            else:
                                sp.wait_ge(b_["new"], at["new"] + 1)
                                settle(sp)
                                sp.dma_start(boundary_rows(tables[L + 1], EP), new[:, :, :]).then_inc(b_["stored"], 16)
                            sp.wait_ge(b_["stored"], at["stored"] + 16)

                    @block.gpsimd
                    def _(q):
                        if ends:
                            q.wait_ge(b_["new"], at["new"] + 1)
                            for j in range(BJ):
                                q.indirect_dma_start(
                                    out=out, out_offset=bass.IndirectOffsetOnAxis(ap=bout[:, j:j + 1], axis=0),
                                    in_=new[:, j, :], in_offset=None,
                                    bounds_check=N - 1, oob_is_err=False).then_inc(b_["scattered"], 16)
                            q.wait_ge(b_["scattered"], 16 * BJ)

                    @block.tensor
                    def _(pe):
                        for j in range(BJ):
                            bank, k = halves(0, j)
                            last = T.transpose(bank[0:BP, k, :], bexp[:, j * BP:(j + 1) * BP], ident[:, :])
                        last.then_inc(b_["rows"], 1)
                        pe.wait_ge(b_["scaled"], v_scaled)
                        for j in range(BJ):
                            to = flat_banks[2 + j // 3][0:BP, (j % 3) * W:(j % 3 + 1) * W]
                            for k in range(BJ):
                                last = T.matmul(to, lhsT=same[:, k, j * BP:(j + 1) * BP], rhs=ex[:, k, :],
                                                start=k == 0, stop=k == BJ - 1)
                        last.then_inc(b_["total"], 1)
                        if not gat:
                            pe.wait_ge(b_["loaded"], n_load)
                            for j in range(BJ):
                                bank, k = halves(0, j)
                                last = T.transpose(bank[:, k, 0:BP], xb[:, j, :], ident[0:BP, 0:BP])
                            last.then_inc(b_["own_t"], 1)
                        pe.wait_ge(b_["sum"], at["sum"] + 1)
                        for j in range(BJ):
                            bank, k = halves(5, j)
                            last = T.transpose(bank[:, k, 0:BP], tot[:, j, :], ident[0:BP, 0:BP])
                        last.then_inc(b_["sum_t"], 1)
                        pe.wait_ge(b_["sum_c"], at["sum_c"] + 1)
                        if not gat:
                            pe.wait_ge(b_["own_c"], at["own_c"] + 1)
                        for h, m in ((0, 4), (1, BJ - 4)):
                            T.matmul(banks[2 + h][0:BP, 0:m, :], lhsT=ones3[:, 0:BP], rhs=brow3[L][:, 0:m, :],
                                     start=True, stop=False, skip_group_check=True)
                            for k in range(m):
                                j = 4 * h + k
                                to = banks[2 + h][0:BP, k, :]
                                if not gat:
                                    T.matmul(to, lhsT=ownT[:, j, :], rhs=wn[l][:, 0, :], start=False, stop=False,
                                             skip_group_check=True)
                                last = T.matmul(to, lhsT=totT[:, j, :], rhs=gat_w[:, l, :] if gat else wn[l][:, 1, :],
                                                start=False, stop=True, skip_group_check=True)
                        last.then_inc(b_["out"], 1)

                    @block.scalar
                    def _(a):
                        if gat:
                            a.wait_ge(b_["max"], at["max"] + 2)
                            S.activation(sc[:, 3, :], sc[:, 4, :], ACT.Exp).then_inc(b_["exp"], 1)
                            a.wait_ge(b_["loaded"], n_load)
                            S.activation(xb[:, :, :], xb[:, :, :], ACT.Copy, bias=0.5).then_inc(b_["half"], 1)
                        a.wait_ge(b_["sum_t"], at["sum_t"] + 1)
                        for h, m in ((0, 4), (1, BJ - 4)):
                            last = S.activation(totT[:, 4 * h:4 * h + m, :], banks[5 + h][:, 0:m, 0:BP], ACT.Copy)
                        last.then_inc(b_["sum_c"], 1)
                        a.wait_ge(b_["out"], at["out"] + 1)
                        for h, m in ((0, 4), (1, BJ - 4)):
                            last = S.activation(act[:, 4 * h:4 * h + m, :], banks[2 + h][0:BP, 0:m, :],
                                                ACT.Tanh if gat else ACT.Relu, scale=0.5 if gat else 1.0)
                        last.then_inc(b_["act"], 1)
                        if zn:
                            norm_scalar_a(a, zn, tn, 1, BP, BJ)
                            norm_scalar_b(a, zn, tn, braw, nrm, 1, BP, BJ)

                    @block.vector
                    def _(v):
                        if gat:
                            v.wait_ge(b_["loaded"], n_load)
                            for j in range(BJ):
                                last = V.tensor_tensor_reduce(out=junk[:, j, :], in0=mrow[:, :], in1=far[:, j, :], scale=1.0,
                                                              scalar=-FAR, op0=ALU.add, op1=ALU.max,
                                                              accum_out=sc[:, 2, j:j + 1])
                            last.then_inc(b_["max"], 1)
                            v.wait_ge(b_["max"], at["max"] + 1)
                            V.tensor_tensor(sc[:, 4, :], sc[:, 0, :], sc[:, 2, :], ALU.subtract).then_inc(b_["max"], 1)
                            v.wait_ge(b_["exp"], at["exp"] + 1)
                            V.tensor_tensor(sc[:, 5, :], sc[:, 3, :], sc[:, 1, :], ALU.mult).then_inc(b_["scale"], 1)
                            v.wait_ge(b_["scale"], at["scale"] + 1)
                        v.wait_ge(b_["rows"], v_rows)
                        for h, m in ((0, 4), (1, BJ - 4)):
                            to, of = ex[:, 4 * h:4 * h + m, 0:C], banks[h][0:BP, 0:m, :]
                            if gat:
                                last = V.tensor_tensor(to, of, sc[:, 5, 4 * h:4 * h + m].unsqueeze(2)
                                                       .broadcast_to([BP, m, C]), ALU.mult)
                            else:
                                last = V.tensor_copy(to, of)
                        if gat:
                            last = V.tensor_copy(ex[:, :, C], sc[:, 5, :])
                        last.then_inc(b_["scaled"], 1)
                        v.wait_ge(b_["total"], at["total"] + 1)
                        sums = [(flat_banks[2 + h][0:BP, 0:m * W].rearrange("p (j w) -> p j w", w=W), 3 * h, m)
                                for h, m in ((0, 3), (1, 3), (2, BJ - 6))]
                        if gat:
                            for of, j, m in sums:
                                last = V.reciprocal(sc[:, 4, j:j + m], of[:, :, C])
                            last.then_inc(b_["inv"], 1)
                            v.wait_ge(b_["inv"], at["inv"] + 1)
                        for of, j, m in sums:
                            if gat:
                                last = V.tensor_tensor(tot[:, j:j + m, :], of[:, :, 0:C],
                                                       sc[:, 4, j:j + m].unsqueeze(2).broadcast_to([BP, m, C]), ALU.mult)
                            else:
                                last = V.tensor_copy(tot[:, j:j + m, :], of[:, :, 0:C])
                        last.then_inc(b_["sum"], 1)
                        if not gat:
                            v.wait_ge(b_["own_t"], at["own_t"] + 1)
                            for h, m in ((0, 4), (1, BJ - 4)):
                                last = V.tensor_copy(ownT[:, 4 * h:4 * h + m, :], banks[h][:, 0:m, 0:BP])
                            last.then_inc(b_["own_c"], 1)
                        v.wait_ge(b_["act"], at["act"] + 1)
                        if gat:
                            v.wait_ge(b_["half"], at["half"] + 1)
                            last = V.scalar_tensor_tensor(out=new[:, :, :], in0=act[:, :, :], scalar=0.5, in1=xb[:, :, :],
                                                          op0=ALU.mult, op1=ALU.add)
                        elif ends:
                            last = V.tensor_tensor(new[:, :, :], act[:, :, :], braw[:, :, :], ALU.add)
                        else:
                            last = V.tensor_copy(new[:, :, :], act[:, :, :])
                        last.then_inc(b_["new"], 1)
                        if zn:
                            v.wait_ge(b_["new"], at["new"] + 1)
                            V.tensor_tensor(braw[:, :, :], braw[:, :, :], new[:, :, :], ALU.add).then_inc(b_["mid"], 1)
                            v.wait_ge(b_["mid"], 1)
                            norm_vector_a(v, zn, tn, braw, 1, BP, BJ)
                            norm_vector_b(v, zn, tn, 1, BP, BJ)
            for k in ("max",):
                b_count[k] += 2 * gat
            for k in ("exp", "half", "scale", "inv"):
                b_count[k] += gat
            for k in ("own_t", "own_c"):
                b_count[k] += not gat
            for k in ("total", "sum", "sum_t", "sum_c", "out", "act", "new"):
                b_count[k] += 1
            b_count["stored"] += 16

        for l in range(LAYERS):
            gat_pass(l)
            boundary_pass(l)
        end_phase(a_.values())
        norm_pass("mid_norm", GE, lambda g: slot_rows(mid_rows, g), lambda g: slot_rows(tables[LAYERS], g), C, 8, 0)
        for l in range(LAYERS):
            net_pass(l)
            boundary_pass(LAYERS + l)
        end_phase()


_RUNS = "x edges edge_w dst_rows src_lookups bnd_rows bnd_cols bnd_numbers slot_numbers node_numbers tail_numbers " \
        "eye gat_w gat_wt att gat_b node_b edge_b bias_rows We0 Wn0 We1 Wn1 We2 Wn2".split()


def laid_out(i):
    def padded(a, fill):
        return np.concatenate([a, np.full(EP - E, fill, a.dtype)])

    src, dst = padded(np.asarray(i["src"]), 0), padded(np.asarray(i["dst"]), N)
    tiles = dst.reshape(-1, P)
    first, last = tiles[:, 0], tiles[:, -1]
    before = np.concatenate([np.full(1, -1, dst.dtype), last[:-1]])
    behind = np.concatenate([first[1:], np.full(1, N, dst.dtype)])

    def columns(a):
        return np.broadcast_to(a.reshape(len(tiles), -1), tiles.shape).T

    def bounds(a, b):
        return np.stack([a.reshape(GE, U), b.reshape(GE, U)], 1).reshape(NB)

    edges = np.stack([columns(a) for a in (dst, src, np.concatenate([dst[1:], behind[-1:]]), first, last, before)], 1)
    bnd = bounds(first, last)
    bnd_cols = np.stack([a.reshape(BJ, BP).T for a in (bnd, bounds(np.full_like(first, -1), first),
                                                       bounds(last, behind))], 1)
    slot = np.arange(EP).reshape(GE, P, U).transpose(1, 0, 2).reshape(P, GE * U)
    ws = np.asarray(i["L0_gnn_Ws"])
    gb = np.asarray(i["L0_gnn_bias"])
    nb = np.stack([np.asarray(i[f"L1_gnn_bn{l}"]) for l in range(LAYERS)])
    eb = np.stack([np.asarray(i[f"L1_gnn_be{l}"]) for l in range(LAYERS)])
    arrays = dict(
        x=np.asarray(i["x"]), edges=edges, edge_w=padded(np.asarray(i["edge_weight"]), 0).reshape(-1, P).T,
        dst_rows=dst.reshape(GE, U, P), src_lookups=src.reshape(GE, U, P).transpose(0, 2, 1),
        bnd_rows=bnd.reshape(1, NB), bnd_cols=bnd_cols,
        bnd_numbers=(EP + np.arange(NB)).reshape(BJ, BP).T.astype(np.float32),
        slot_numbers=slot.astype(np.float32),
        node_numbers=(NODE0 + np.arange(P * U)).reshape(P, U).astype(np.float32),
        tail_numbers=(NODE0 + GN * P * U + np.arange(TAIL)).reshape(TP, TU).astype(np.float32),
        eye=np.eye(P, dtype=np.float32), gat_w=ws.transpose(1, 0, 2), gat_wt=ws.transpose(2, 0, 1),
        att=np.concatenate([np.asarray(i["L0_gnn_att_src"]), np.asarray(i["L0_gnn_att_dst"])]).T,
        gat_b=gb.T, node_b=nb.T, edge_b=eb.T,
        bias_rows=np.broadcast_to(np.concatenate([gb, nb]), (3, 2 * LAYERS, C)))
    for l in range(LAYERS):
        arrays[f"We{l}"] = np.asarray(i[f"L1_gnn_We{l}"])
        arrays[f"Wn{l}"] = np.asarray(i[f"L1_gnn_Wn{l}"])
    return {k: np.ascontiguousarray(v) for k, v in arrays.items()}


def kernel(**inputs):
    import concourse.bacc as _bacc
    from concourse import mybir as _mybir
    from concourse.bass_utils import run_bass_kernel_spmd as _run

    nc = _bacc.Bacc("TRN2", target_bir_lowering=False, num_devices=1)
    laid = laid_out(inputs)
    arrays, args = {}, []
    for name in _RUNS:
        a = laid[name]
        arrays[f"in_{name}_dram"] = a
        args.append(nc.dram_tensor(f"in_{name}_dram", a.shape, _mybir.dt.from_np(a.dtype), kind="ExternalInput").ap())
    args.append(nc.dram_tensor("out_0_dram", (N, C), _mybir.dt.from_np(np.dtype("float32")), kind="ExternalOutput").ap())
    build(nc, *args)
    r = _run(nc, [arrays], core_ids=[0])
    return r.results[0]["out_0_dram"]
```
